# Optimizing a Trainium2 kernel written in Bass

```python
import numpy as np
import jax
import jax.numpy as jnp

def _softmax(x, axis=-1):
    return jax.nn.softmax(x, axis=axis)

def _gelu(x):
    return jax.nn.gelu(x, approximate=True)

def _silu(x):
    return jax.nn.silu(x)

def _sigmoid(x):
    return jax.nn.sigmoid(x)

def _layernorm(x, axis=-1, eps=1e-05):
    m = jnp.mean(x, axis=axis, keepdims=True)
    v = jnp.var(x, axis=axis, keepdims=True)
    return (x - m) / jnp.sqrt(v + eps)

def _scatter_add(tgt, idx, src, axis=0):
    return tgt.at[idx].add(src)

def _segment_sum(src, seg, n):
    return jax.ops.segment_sum(src, seg, n)
kernel_name = 'mk_flamingo_gated_d1_seqx_r8_948102'

def setup_inputs(seed: int=0):
    np.random.seed(seed)
    _w = jnp.asarray

    def _rec_inputs():
        import jax
        import jax.numpy as jnp
        _rk = jax.random.key(seed)
        x = -0.0002928 + 1 * jax.random.normal(jax.random.fold_in(_rk, 1), (16, 256, 128), jnp.float32)
        _lenS = 256 - jax.random.randint(jax.random.fold_in(_rk, 7), (16,), 0, max(1, 256 // 4) + 1, jnp.int32)
        _lenS2 = 1601 - jax.random.randint(jax.random.fold_in(_rk, 8), (16,), 0, max(1, 1601 // 4) + 1, jnp.int32)
        _ctx_1024P = jax.random.normal(jax.random.fold_in(_rk, 11), (16, 16, 128), jnp.float32)
        _ctx_1024c = jax.random.dirichlet(jax.random.fold_in(_rk, 511), 0.3 * jnp.ones((16,), jnp.float32), (16, 1601))
        _ctx_1024t = jnp.einsum('bsk,bkd->bsd', _ctx_1024c, _ctx_1024P)
        _ctx_1024t = _ctx_1024t * jax.lax.rsqrt(jnp.mean(jnp.square(_ctx_1024t)) + 1e-12) * 0.953939
        ctx_1024 = -1.39393e-06 + 0.999914 * (_ctx_1024t + 0.3 * jax.random.normal(jax.random.fold_in(_rk, 611), (16, 1601, 128), jnp.float32))
        _g = jax.random.normal(jax.random.fold_in(_rk, 9001), (2, 1), jnp.float32)
        _g = jnp.sign(_g) * jnp.maximum(jnp.abs(_g), 1.0) + (_g == 0) * 1.0
        g_xattn = _g[0]
        g_ffn = _g[1]
        return (x, ctx_1024, g_xattn, g_ffn)
    x, ctx_1024, g_xattn, g_ffn = _rec_inputs()

    def _L0_xattn_setup():
        import jax, jax.numpy as jnp
        import numpy as np
        SCALE = 0.125
        key = jax.random.key(seed)
        ks = jax.random.split(key, 7)
        B, N, Dq, Dkv, H = (2, 256, 128, 128, 16)
        Dh = Dq // H
        return {'q': jax.random.normal(ks[0], (B, N, Dq), dtype=jnp.float32), 'k': jax.random.normal(ks[1], (B, N, Dkv), dtype=jnp.float32), 'v': jax.random.normal(ks[2], (B, N, Dkv), dtype=jnp.float32), 'Wq': jax.random.normal(ks[3], (H, Dq, Dh), dtype=jnp.float32) * 0.02, 'Wk': jax.random.normal(ks[4], (H, Dkv, Dh), dtype=jnp.float32) * 0.02, 'Wv': jax.random.normal(ks[5], (H, Dkv, Dh), dtype=jnp.float32) * 0.02, 'Wo': jax.random.normal(ks[6], (Dq, Dq), dtype=jnp.float32) * 0.02}
    _L0_xattn_all = _L0_xattn_setup()
    _L0_xattn_in = {k: v for k, v in _L0_xattn_all.items() if k in ('Wq', 'Wk', 'Wv', 'Wo')}
    del _L0_xattn_all

    def _L0_ffn_setup():
        import jax, jax.numpy as jnp
        import numpy as np
        N_EMBD = 128
        NUM_EXPERTS = 8
        TOP_K = 2

        def new_gelu(x):
            c = jnp.sqrt(2.0 / jnp.pi).astype(x.dtype)
            return 0.5 * x * (1.0 + jnp.tanh(c * (x + 0.044715 * x ** 3)))
        key = jax.random.key(seed)
        ks = jax.random.split(key, 6)
        C, E, H = (N_EMBD, NUM_EXPERTS, 4 * N_EMBD)
        x = jax.random.normal(ks[0], (4, 256, C), dtype=jnp.float32)
        router_w = 0.02 * jax.random.normal(ks[1], (E, C), dtype=jnp.float32)
        w1 = 0.02 * jax.random.normal(ks[2], (E, H, C), dtype=jnp.float32)
        b1 = jnp.zeros((E, H), dtype=jnp.float32)
        w2 = 0.02 * jax.random.normal(ks[3], (E, C, H), dtype=jnp.float32)
        b2 = jnp.zeros((E, C), dtype=jnp.float32)
        return {'x': x, 'router_w': router_w, 'w1': w1, 'b1': b1, 'w2': w2, 'b2': b2}
    _L0_ffn_all = _L0_ffn_setup()
    _L0_ffn_in = {k: v for k, v in _L0_ffn_all.items() if k in ('router_w', 'w1', 'b1', 'w2', 'b2')}
    del _L0_ffn_all
    return {'x': x, 'ctx_1024': ctx_1024, 'g_xattn': g_xattn, 'g_ffn': g_ffn, 'L0_xattn_Wq': _L0_xattn_in['Wq'], 'L0_xattn_Wk': _L0_xattn_in['Wk'], 'L0_xattn_Wv': _L0_xattn_in['Wv'], 'L0_xattn_Wo': _L0_xattn_in['Wo'], 'L0_ffn_router_w': _L0_ffn_in['router_w'], 'L0_ffn_w1': _L0_ffn_in['w1'], 'L0_ffn_b1': _L0_ffn_in['b1'], 'L0_ffn_w2': _L0_ffn_in['w2'], 'L0_ffn_b2': _L0_ffn_in['b2']}

def reference(x, ctx_1024, g_xattn, g_ffn, L0_xattn_Wq, L0_xattn_Wk, L0_xattn_Wv, L0_xattn_Wo, L0_ffn_router_w, L0_ffn_w1, L0_ffn_b1, L0_ffn_w2, L0_ffn_b2):
    import jax
    import jax.numpy as jnp

    def _L0_xattn_ref(q, k, v, Wq, Wk, Wv, Wo):
        import jax, jax.numpy as jnp
        import numpy as np
        SCALE = 0.125
        qh = jnp.einsum('bnd,hde->bhne', q, Wq)
        kh = jnp.einsum('bmd,hde->bhme', k, Wk)
        vh = jnp.einsum('bmd,hde->bhme', v, Wv)
        scores = jnp.einsum('bhne,bhme->bhnm', qh, kh) * SCALE
        att = jax.nn.softmax(scores, axis=-1)
        out_h = jnp.einsum('bhnm,bhme->bhne', att, vh)
        B, H, N, Dh = out_h.shape
        concat = out_h.transpose(0, 2, 1, 3).reshape(B, N, H * Dh)
        return jnp.einsum('bnd,od->bno', concat, Wo)

    def _L0_ffn_ref(x, router_w, w1, b1, w2, b2):
        import jax, jax.numpy as jnp
        import numpy as np
        N_EMBD = 128
        NUM_EXPERTS = 8
        TOP_K = 2

        def new_gelu(x):
            c = jnp.sqrt(2.0 / jnp.pi).astype(x.dtype)
            return 0.5 * x * (1.0 + jnp.tanh(c * (x + 0.044715 * x ** 3)))
        B, T, C = x.shape
        E = router_w.shape[0]
        x_flat = x.reshape(B * T, C)
        router_logits = x_flat @ router_w.T
        router_probs = jax.nn.softmax(router_logits, axis=-1)
        top_k_probs, top_k_idx = jax.lax.top_k(router_probs, TOP_K)
        top_k_probs = top_k_probs / (top_k_probs.sum(axis=-1, keepdims=True) + 1e-08)
        cw = (jax.nn.one_hot(top_k_idx, E, dtype=x.dtype) * top_k_probs[..., None]).sum(axis=1)
        output = jnp.zeros_like(x_flat)
        for e in range(E):
            h = new_gelu(x_flat @ w1[e].T + b1[e])
            out_e = h @ w2[e].T + b2[e]
            output = output + cw[:, e:e + 1] * out_e
        return output.reshape(B, T, C)
    x = x + jnp.tanh(g_xattn[0]) * _L0_xattn_ref(_layernorm(x, axis=-1), ctx_1024, ctx_1024, L0_xattn_Wq, L0_xattn_Wk, L0_xattn_Wv, L0_xattn_Wo)
    x = x + jnp.tanh(g_ffn[0]) * _L0_ffn_ref(_layernorm(x, axis=-1), L0_ffn_router_w, L0_ffn_w1, L0_ffn_b1, L0_ffn_w2, L0_ffn_b2)
    return x

_drawn_inputs = setup_inputs


def setup_inputs(seed=0):
    import zlib

    import numpy as np

    out = dict(_drawn_inputs(seed))
    spreads = {'L0_ffn_b1': (0.0, 0.491), 'L0_ffn_b2': (0.0, 0.1)}
    factors = {'ctx_1024': 2.91, 'L0_xattn_Wq': 8.0, 'L0_xattn_Wk': 8.0}
    for name, (base, spread) in spreads.items():
        noise = np.random.default_rng([zlib.crc32(name.encode()), seed]).standard_normal(out[name].shape)
        drawn = base * np.exp(spread * noise) if base else spread * noise
        out[name] = jnp.asarray(drawn.astype(out[name].dtype))
    for name, factor in factors.items():
        out[name] = (out[name] * factor).astype(out[name].dtype)
    return out
```

```python
import math
from contextlib import ExitStack

import concourse.bass as bass
import numpy as np
from concourse import mybir

F32 = mybir.dt.float32
F32R = mybir.dt.float32r
ALU = mybir.AluOpType
ACT = mybir.ActivationFunctionType
AX = mybir.AxisListType

B, N, D = 16, 256, 128
M = 1601
H, DH = 16, 8
NE, HID = 8, 512
P = 128
SCALE = 0.125
LN_EPS = 1e-5
TOPK_EPS = 1e-8

NT = N // P
TILES = B * NT
HG = 4
NG = H // HG
KT = -(-M // P)
UNITS = NG * KT
WIN = 402
WSTART = [0, 400, 800, M - WIN]
NW = len(WSTART)
KCH = [(0, 401), (401, 400), (801, 400), (1201, 400)]
VCH = [(0, 4), (4, 4), (8, 4), (12, 1)]
VC = DH + 1
VW = VC * (H - 1) + 32
PARTS = 3
MAXROW = PARTS * HG * DH
SCORE_ROWS = MAXROW + 2
LAG = 2
ST_BUFS = 3
PT_BUFS = 6
BLK = 512
NBLK = B * N // BLK
BT = BLK // P
HC = HID // P


def key_rows(kt):
    return min(P, M - kt * P)


def schedule():
    ev = []

    def maxima(G, first, last):
        for m in range(first, last):
            ev.append(("MX", G, m))
        if last == HG * NT * NW:
            ev.append(("MF", G))

    n_max = HG * NT * NW
    ev += [("X", 0), ("Q", 0)] + [("K", 0, c) for c in range(len(KCH))]
    ev += [("V", 0, c) for c in range(len(VCH))]
    maxima(0, 0, n_max)
    ev.append(("MT", 0))
    maxima(1, 0, n_max)
    for u in range(B * UNITS):
        b, r = divmod(u, UNITS)
        g, kt = divmod(r, KT)
        G = b * NG + g
        lo, hi = kt * n_max // KT, (kt + 1) * n_max // KT
        if G + 2 >= B * NG:
            lo = hi = 0
        ev.append(("S", u, 0))
        if hi > lo:
            maxima(G + 2, lo, lo + 1)
        ev.append(("S", u, 1))
        if hi > lo:
            maxima(G + 2, lo + 1, hi - 1 if hi - lo > 2 else hi)
        if u >= LAG:
            ev.append(("PV", u - LAG))
        if hi - lo > 2:
            maxima(G + 2, hi - 1, hi)
        if kt == 2 and G + 1 < B * NG:
            ev.append(("MT", G + 1))
        if b + 1 < B:
            if r == 0:
                ev.append(("X", b + 1))
            if r == 4:
                ev.append(("Q", b + 1))
            if 11 <= r < 11 + len(KCH):
                ev.append(("K", b + 1, r - 11))
            if r in (30, 32, 34, 36):
                ev.append(("V", b + 1, (r - 30) // 2))
        if b > 0:
            if r == 5:
                ev.append(("F1", b - 1))
            if r == 7:
                ev.append(("F2", b - 1))
            if r == 9:
                ev.append(("F3", b - 1))
    for u in range(B * UNITS - LAG, B * UNITS):
        ev.append(("PV", u))
    ev += [("F1", B - 1), ("F2", B - 1), ("F3", B - 1)]
    return ev


MISC = ("X", "Q", "K", "V", "MT", "F1", "F2", "F3")


def build(nc, x, ctxT, gates, wq, wk, wv, woT, rwT, w1T, b1T, w2T, b2, ident, sel, out):
    events = schedule()
    misc_no = {}
    for e in events:
        if e[0] in MISC:
            misc_no[e] = len(misc_no)

    ctx = ExitStack()
    with ctx:
        def sb(name, shape, dt=F32):
            return ctx.enter_context(nc.sbuf_tensor(name, shape, dt))

        def sem(name):
            return ctx.enter_context(nc.semaphore(name))

        x_sb = sb("x_sb", [P, TILES, D])
        ARENA = 2 * M + 2 * KT * VW + PT_BUFS * BLK
        arena = sb("arena", [P, ARENA])
        at = 0
        ctx_sb = arena[:, at:at + 2 * M].rearrange("p (k m) -> p k m", k=2)
        at += 2 * M
        vaug = arena[:, at:at + 2 * KT * VW].rearrange("p (k t w) -> p k t w", k=2, t=KT)
        at += 2 * KT * VW
        pt = arena[:, at:at + PT_BUFS * BLK].rearrange("p (k n) -> p k n", k=PT_BUFS)
        at = 0
        hid = arena[:, at:at + 2 * HC * BLK].rearrange("p (k c n) -> p k c n", k=2, c=HC)
        at += 2 * HC * BLK
        xn2T = arena[:, at:at + NBLK * BLK].rearrange("p (k n) -> p k n", k=NBLK)
        at += NBLK * BLK
        xn2 = arena[:, at:at + 2 * BLK].rearrange("p (k t d) -> p k t d", k=2, t=BT)
        at += 2 * BLK
        acc = arena[:, at:at + BLK].rearrange("p (t d) -> p t d", t=BT)
        at += BLK
        assert at <= ARENA
        kpack = sb("kpack", [P, 2, NG, M], F32R)
        khl = sb("khl", [P, 2, M], F32R)
        qmask = sb("qmask", [P, 2, NG, HG, N], F32R)
        qhl = sb("qhl", [P, 2, N], F32R)
        wq_sb, wk_sb, wv_sb, wo_sb = (sb(n, [P, D]) for n in ("wq_sb", "wk_sb", "wv_sb", "wo_sb"))
        id_sb = sb("id_sb", [P, P])
        sel_sb = sb("sel_sb", [P, HG * VC])
        rw_sb = sb("rw_sb", [P, NE])
        w1_sb = sb("w1_sb", [P, NE * HID])
        w2_sb = sb("w2_sb", [P, NE * HC, D])
        b1_sb = sb("b1_sb", [P, NE * HC])
        b2_sb = sb("b2_sb", [P, NE, D])
        gate = sb("gate", [P, 2])
        tgate = sb("tgate", [P, 2])
        xn = sb("xn", [P, NT, D])
        xnT = sb("xnT", [P, N])
        pv_sb = sb("pv_sb", [P, 2, BLK])
        conc = sb("conc", [P, NT, H, DH])
        concT = sb("concT", [P, N])
        rden = sb("rden", [P, NT * H])
        mx = sb("mx", [P, 2, NT * HG, NW])
        nmx = sb("nmx", [P, NT * HG])
        mxhl = sb("mxhl", [P, NT, 2, HG], F32R)
        mxT = sb("mxT", [2 * HG, N], F32R)
        bst = sb("bst", [P, 2, 6])
        stat = sb("stat", [P, TILES, 2])
        rstd = sb("rstd", [P, TILES])
        nmr = sb("nmr", [P, TILES])
        tmp = sb("tmp", [P, TILES])
        var = sb("var", [P, TILES])
        lg = sb("lg", [P, TILES, NE])
        eq = sb("eq", [P, TILES, NE])
        oh1 = sb("oh1", [P, TILES, NE])
        cw = sb("cw", [P, TILES, NE])
        top = sb("top", [P, 3, TILES])
        rank = sb("rank", [P, NE])

        bank = [ctx.enter_context(nc.psum_tensor(f"bank{i}", [P, BLK], F32)) for i in range(8)]
        st, mxp, pv, misc = bank[0:3], bank[3:5], bank[5:7], bank[7]

        s_w = sem("s_w")
        s_x = [sem(f"s_x{q}") for q in range(4)]
        s_ffw = sem("s_ffw")
        s_ctx = [sem("s_ctx0"), sem("s_ctx1")]
        s_fill = sem("s_fill")
        s_init = sem("s_init")
        s_rstd = sem("s_rstd")
        s_sqrt = sem("s_sqrt")
        s_var = sem("s_var")
        s_tanh = sem("s_tanh")
        s_xn = sem("s_xn")
        s_misc = sem("s_misc")
        s_xnT = sem("s_xnT")
        s_qhi = sem("s_qhi")
        s_qlo = sem("s_qlo")
        s_khi = sem("s_khi")
        s_klo = sem("s_klo")
        s_qd = [sem("s_qd0"), sem("s_qd1")]
        s_kd = [sem("s_kd0"), sem("s_kd1")]
        s_v = sem("s_v")
        s_mxp = sem("s_mxp")
        s_red = sem("s_red")
        s_mxhl = sem("s_mxhl")
        s_mxT = sem("s_mxT")
        s_mxd = [sem("s_mxd0"), sem("s_mxd1")]
        s_st = sem("s_st")
        s_exp = sem("s_exp")
        s_pv = sem("s_pv")
        s_pvs = sem("s_pvs")
        s_conc = sem("s_conc")
        s_concT = sem("s_concT")
        s_dve = sem("s_dve")
        s_res = sem("s_res")
        s_xn2 = sem("s_xn2")
        s_tr = sem("s_tr")
        s_trf = sem("s_trf")
        s_rt = sem("s_rt")
        s_lg = sem("s_lg")
        s_pe = sem("s_pe")
        s_cw = sem("s_cw")
        s_hp = sem("s_hp")
        s_hg = sem("s_hg")
        s_y = sem("s_y")
        s_bias = sem("s_bias")
        s_add = sem("s_add")
        s_o = sem("s_o")
        s_out = sem("s_out")

        signal = {"X": s_xnT, "Q": s_qlo, "K": s_klo, "V": s_v, "MT": s_mxT, "F1": s_conc,
                  "F2": s_concT, "F3": s_res}
        uses = dict.fromkeys(signal, 0)
        read_out = []
        for e in misc_no:
            uses[e[0]] += 1
            read_out.append((signal[e[0]], uses[e[0]]))

        block = ctx.enter_context(nc.Block())

        def waiter(eng):
            seen = {}

            def wait(s, value):
                if value > seen.get(id(s), 0):
                    seen[id(s)] = value
                    eng.wait_ge(s, value)
            return wait

        @block.sync
        def _(eng):
            wait = waiter(eng)
            n_w = 0
            for dst, src in ((wk_sb, wk), (wv_sb, wv), (wq_sb, wq), (id_sb, ident)):
                eng.dma_start(dst[:, :], src).then_inc(s_w, 16)
                n_w += 1
            xs = x.rearrange("(t p) d -> p t d", p=P)
            for q in range(4):
                t0, t1 = q * TILES // 4, (q + 1) * TILES // 4
                eng.dma_start(x_sb[:, t0:t1, :], xs[:, t0:t1, :]).then_inc(s_x[q], 16)
                if q == 0:
                    eng.dma_start(ctx_sb[:, 0, :], ctxT[0]).then_inc(s_ctx[0], 16)
            for dst, src in ((wo_sb, woT), (sel_sb, sel), (rw_sb, rwT), (b1_sb, b1T)):
                eng.dma_start(dst[:, :], src).then_inc(s_w, 16)
                n_w += 1
            eng.dma_start(gate[:, :], gates.partition_broadcast(P)).then_inc(s_w, 16)
            eng.dma_start(ctx_sb[:, 1, :], ctxT[1]).then_inc(s_ctx[1], 16)
            assert n_w + 1 == N_W
            for e in events:
                if e[0] == "Q":
                    b = e[1]
                    if b == 0:
                        wait(s_fill, 2)
                    wait(s_qlo, b + 1)
                    wait(s_st, 2 * UNITS * (b - 1))
                    for part, hl in enumerate((0, 0, 1)):
                        for h in range(H):
                            g, j = divmod(h, HG)
                            r = part * HG * DH + j * DH
                            eng.dma_start(qmask[r:r + DH, b % 2, g, j, :].bitcast(F32),
                                          qhl[h * DH:(h + 1) * DH, hl, :].bitcast(F32)
                                          ).then_inc(s_qd[b % 2], 16)
                elif e[0] == "K" and e[2] == len(KCH) - 1:
                    b = e[1]
                    wait(s_klo, len(KCH) * (b + 1))
                    wait(s_st, 2 * UNITS * (b - 1))
                    for g in range(NG):
                        for part, hl in enumerate((0, 1, 0)):
                            r = part * HG * DH
                            eng.dma_start(kpack[r:r + HG * DH, b % 2, g, :].bitcast(F32),
                                          khl[g * HG * DH:(g + 1) * HG * DH, hl, :].bitcast(F32)
                                          ).then_inc(s_kd[b % 2], 16)
                elif e[0] == "V" and e[2] == len(VCH) - 1:
                    b = e[1]
                    if b + 2 < B:
                        wait(s_v, len(VCH) * (b + 1))
                        eng.dma_start(ctx_sb[:, b % 2, :], ctxT[b + 2]).then_inc(s_ctx[b % 2], 16)
                    if b == 0:
                        for dst, src in ((w1_sb[:, :], w1T),
                                         (w2_sb[:, :, :], w2T),
                                         (b2_sb[:, :, :].rearrange("p e d -> p (e d)"),
                                          b2.partition_broadcast(P))):
                            eng.dma_start(dst, src).then_inc(s_ffw, 16)
                elif e[0] == "MT":
                    b, g = divmod(e[1], NG)
                    wait(s_mxT, e[1] + 1)
                    for hl in range(2):
                        eng.dma_start(
                            qmask[MAXROW + hl:MAXROW + hl + 1, b % 2, g, :, :].bitcast(F32),
                            mxT[hl * HG:(hl + 1) * HG, :].bitcast(F32)
                        ).then_inc(s_mxd[e[1] % 2], 16)
            outs = out.rearrange("(t p) d -> p t d", p=P)
            for k in range(NBLK):
                wait(s_o, k + 1)
                eng.dma_start(outs[:, k * BT:(k + 1) * BT, :],
                              x_sb[:, k * BT:(k + 1) * BT, :]).then_inc(s_out, 16)
            eng.wait_ge(s_out, 16 * NBLK)

        @block.gpsimd
        def _(eng):
            wait = waiter(eng)
            eng.memset(kpack[MAXROW:P, :, :, :].bitcast(F32), 1.0).then_inc(s_fill, 1)
            wait(s_fill, 1)
            eng.memset(qmask[:, :, :, :, :].bitcast(F32), 0.0).then_inc(s_fill, 1)
            for e in events:
                if e[0] == "X":
                    b = e[1]
                    wait(s_rstd, 1)
                    wait(s_misc, misc_no[("X", b - 1)] + 1 if b else 0)
                    for t in range(NT):
                        i = b * NT + t
                        eng.tensor_scalar(xn[:, t, :], x_sb[:, i, :], rstd[:, i:i + 1],
                                          nmr[:, i:i + 1], ALU.mult, ALU.add).then_inc(s_xn, 1)
            wait(s_rstd, 2)
            for k in range(NBLK):
                wait(s_tr, k - 1)
                for t in range(BT):
                    i = k * BT + t
                    eng.tensor_scalar(xn2[:, k % 2, t, :], x_sb[:, i, :], rstd[:, i:i + 1],
                                      nmr[:, i:i + 1], ALU.mult, ALU.add).then_inc(s_xn2, 1)

        @block.tensor
        def _(eng):
            wait = waiter(eng)

            def misc_bank(e):
                if misc_no[e]:
                    wait(*read_out[misc_no[e] - 1])

            n_mx = 0
            wait(s_w, 16 * N_W)
            for e in events:
                kind = e[0]
                if kind == "S":
                    u, p = e[1:]
                    b, r = divmod(u, UNITS)
                    g, kt = divmod(r, KT)
                    G, c, n = b * NG + g, 2 * u + p, key_rows(kt)
                    wait(s_mxd[G % 2], 32 * (G // 2 + 1))
                    wait(s_exp, c - ST_BUFS + 1)
                    eng.matmul(st[c % ST_BUFS][0:n, :],
                               kpack[0:SCORE_ROWS, b % 2, g, kt * P:kt * P + n],
                               qmask[0:SCORE_ROWS, b % 2, g, 2 * p:2 * p + 2, :],
                               start=True, stop=True).then_inc(s_st, 1)
                elif kind == "MX":
                    G, m = e[1:]
                    b, g = divmod(G, NG)
                    tj, w = divmod(m, NW)
                    t, j = divmod(tj, HG)
                    if m == 0:
                        wait(s_qd[b % 2], 16 * PARTS * H * (b // 2 + 1))
                        wait(s_kd[b % 2], 16 * PARTS * NG * (b // 2 + 1))
                    wait(s_red, n_mx - 1)
                    eng.matmul(mxp[n_mx % 2][:, 0:WIN],
                               qmask[0:MAXROW, b % 2, g, j, t * P:(t + 1) * P],
                               kpack[0:MAXROW, b % 2, g, WSTART[w]:WSTART[w] + WIN],
                               start=True, stop=True).then_inc(s_mxp, 1)
                    n_mx += 1
                elif kind == "MT":
                    misc_bank(e)
                    wait(s_mxhl, e[1] + 1)
                    for t in range(NT):
                        ins = eng.matmul(misc[0:2 * HG, t * P:(t + 1) * P],
                                         mxhl[:, t, :, :].rearrange("p s j -> p (s j)").bitcast(F32),
                                         id_sb[:, :], start=True, stop=True)
                    ins.then_inc(s_misc, 1)
                elif kind == "PV":
                    u = e[1]
                    b, r = divmod(u, UNITS)
                    g, kt = divmod(r, KT)
                    n = key_rows(kt)
                    wait(s_v, len(VCH) * (b + 1))
                    wait(s_pvs, b * (NG // 2) + g // 2 - 1)
                    for j in range(HG):
                        if j % 2 == 0:
                            wait(s_exp, 2 * u + j // 2 + 1)
                        h = g * HG + j
                        ins = eng.matmul(
                            pv[g // 2][32 * j:32 * j + 32, (g % 2) * N:(g % 2 + 1) * N],
                            vaug[0:n, b % 2, kt, VC * h:VC * h + 32],
                            pt[0:n, (2 * u + j // 2) % PT_BUFS, (j % 2) * N:(j % 2 + 1) * N],
                            start=(kt == 0), stop=(kt == KT - 1), tile_position=(0, 32 * j))
                    ins.then_inc(s_pv, 1)
                elif kind == "X":
                    misc_bank(e)
                    wait(s_xn, NT * (e[1] + 1))
                    for t in range(NT):
                        ins = eng.transpose(misc[:, t * P:(t + 1) * P], xn[:, t, :], id_sb[:, :])
                    ins.then_inc(s_misc, 1)
                elif kind == "Q":
                    misc_bank(e)
                    wait(s_xnT, e[1] + 1)
                    eng.matmul(misc[:, 0:N], wq_sb[:, :], xnT[:, :],
                               start=True, stop=True).then_inc(s_misc, 1)
                elif kind == "K":
                    b, c = e[1:]
                    k0, kn = KCH[c]
                    misc_bank(e)
                    wait(s_ctx[b % 2], 16 * (b // 2 + 1))
                    eng.matmul(misc[:, 0:kn], wk_sb[:, :], ctx_sb[:, b % 2, k0:k0 + kn],
                               start=True, stop=True).then_inc(s_misc, 1)
                elif kind == "V":
                    b, c = e[1:]
                    misc_bank(e)
                    t0, tn = VCH[c]
                    for i in range(tn):
                        n = key_rows(t0 + i)
                        ins = eng.matmul(misc[0:n, i * D:(i + 1) * D],
                                         ctx_sb[:, b % 2, (t0 + i) * P:(t0 + i) * P + n],
                                         wv_sb[:, :], start=True, stop=True)
                    ins.then_inc(s_misc, 1)
                elif kind == "F1":
                    b = e[1]
                    misc_bank(e)
                    wait(s_pvs, 2 * (b + 1))
                    for t in range(NT):
                        for g in range(NG):
                            c0 = (g % 2) * N + t * P
                            ins = eng.matmul(
                                misc[:, (t * NG + g) * HG * VC:(t * NG + g + 1) * HG * VC],
                                pv_sb[:, g // 2, c0:c0 + P], sel_sb[:, :], start=True, stop=True)
                    ins.then_inc(s_misc, 1)
                elif kind == "F2":
                    misc_bank(e)
                    wait(s_conc, e[1] + 1)
                    for t in range(NT):
                        ins = eng.transpose(misc[:, t * P:(t + 1) * P],
                                            conc[:, t, :, :].rearrange("p h e -> p (h e)"),
                                            id_sb[:, :])
                    ins.then_inc(s_misc, 1)
                elif kind == "F3":
                    misc_bank(e)
                    wait(s_concT, e[1] + 1)
                    for t in range(NT):
                        ins = eng.matmul(misc[:, t * P:(t + 1) * P], concT[:, t * P:(t + 1) * P],
                                         wo_sb[:, :], start=True, stop=True)
                    ins.then_inc(s_misc, 1)

            logits = mxp[1]
            wait(s_red, n_mx)
            for k in range(NBLK):
                wait(s_xn2, BT * (k + 1))
                if k == 0:
                    wait(*read_out[-1])
                wait(s_trf, k)
                for t in range(BT):
                    ins = eng.transpose(misc[:, t * P:(t + 1) * P], xn2[:, k % 2, t, :], id_sb[:, :])
                ins.then_inc(s_tr, 1)
                if k > 0:
                    for t in range(BT):
                        i = (k - 1) * BT + t
                        ins = eng.matmul(logits[:, i * NE:(i + 1) * NE],
                                         xn2T[:, k - 1, t * P:(t + 1) * P], rw_sb[:, :],
                                         start=True, stop=True)
            wait(s_trf, NBLK)
            for t in range(BT):
                i = (NBLK - 1) * BT + t
                ins = eng.matmul(logits[:, i * NE:(i + 1) * NE],
                                 xn2T[:, NBLK - 1, t * P:(t + 1) * P], rw_sb[:, :],
                                 start=True, stop=True)
            ins.then_inc(s_rt, 1)

            wait(s_ffw, 48)
            hp, yp = [st[0], st[1], st[2], mxp[0]], pv
            for i in range(NBLK * NE + 1):
                for c in range(HC):
                    if i < NBLK * NE:
                        k, ex = divmod(i, NE)
                        wait(s_hg, HC * (i - 1) + c + 1)
                        eng.matmul(hp[c][:, :], w1_sb[:, (ex * HC + c) * P:(ex * HC + c + 1) * P],
                                   xn2T[:, k, :], start=True, stop=True).then_inc(s_hp, 1)
                    if i > 0:
                        q = i - 1
                        t = c
                        wait(s_hg, HC * (q + 1))
                        wait(s_add, BT * (q - 1))
                        for cc in range(HC):
                            ins = eng.matmul(yp[q % 2][:, t * D:(t + 1) * D],
                                             hid[:, q % 2, cc, t * P:(t + 1) * P],
                                             w2_sb[:, (q % NE) * HC + cc, :],
                                             start=(cc == 0), stop=(cc == HC - 1))
                        if t == BT - 1:
                            ins.then_inc(s_y, 1)

        @block.scalar
        def _(eng):
            wait = waiter(eng)
            wait(s_var, 1)
            eng.activation(rstd[:, :], var[:, :], ACT.Sqrt).then_inc(s_sqrt, 1)
            wait(s_w, 16 * N_W)
            eng.activation(tgate[:, :], gate[:, :], ACT.Tanh).then_inc(s_tanh, 1)
            for e in events:
                kind = e[0]
                if kind == "S":
                    u, p = e[1:]
                    c, n = 2 * u + p, key_rows(u % KT)
                    wait(s_st, c + 1)
                    wait(s_pv, (c - PT_BUFS) // 2 + 1)
                    eng.activation(pt[0:n, c % PT_BUFS, :], st[c % ST_BUFS][0:n, :], ACT.Exp,
                                   scale=SCALE).then_inc(s_exp, 1)
                elif kind == "PV":
                    b, r = divmod(e[1], UNITS)
                    if r % (2 * KT) == 2 * KT - 1:
                        wait(s_pv, e[1] + 1)
                        if b > 0:
                            wait(s_misc, misc_no[("F1", b - 1)] + 1)
                        i = r // (2 * KT)
                        eng.activation(pv_sb[:, i, :], pv[i][:, :], ACT.Copy).then_inc(s_pvs, 1)
                elif kind == "X":
                    wait(s_misc, misc_no[e] + 1)
                    eng.activation(xnT[:, :], misc[:, 0:N], ACT.Copy).then_inc(s_xnT, 1)
                elif kind == "Q":
                    b = e[1]
                    wait(s_misc, misc_no[e] + 1)
                    if b > 0:
                        wait(s_qd[(b - 1) % 2], 16 * PARTS * H * ((b - 1) // 2 + 1))
                    eng.activation(qhl[:, 0, :], misc[:, 0:N], ACT.Copy).then_inc(s_qhi, 1)
                elif kind == "K":
                    b, c = e[1:]
                    k0, kn = KCH[c]
                    wait(s_misc, misc_no[e] + 1)
                    if b > 0 and c == 0:
                        wait(s_kd[(b - 1) % 2], 16 * PARTS * NG * ((b - 1) // 2 + 1))
                    eng.activation(khl[:, 0, k0:k0 + kn], misc[:, 0:kn], ACT.Copy).then_inc(s_khi, 1)
                elif kind == "V":
                    b, c = e[1:]
                    t0, tn = VCH[c]
                    n = key_rows(t0 + tn - 1)
                    wait(s_misc, misc_no[e] + 1)
                    wait(s_pv, UNITS * (b - 1))
                    if b == 0:
                        wait(s_init, N_INIT)
                    eng.activation(
                        vaug[0:n, b % 2, t0:t0 + tn, 0:VC * H]
                        .rearrange("p t (h c) -> p t h c", c=VC)[:, :, :, 0:DH],
                        misc[0:n, 0:tn * D].rearrange("p (t h e) -> p t h e", t=tn, e=DH),
                        ACT.Copy).then_inc(s_v, 1)
                elif kind == "MT":
                    G = e[1]
                    wait(s_misc, misc_no[e] + 1)
                    if G > 0:
                        wait(s_mxd[(G - 1) % 2], 32 * ((G - 1) // 2 + 1))
                    eng.activation(mxT[:, :], misc[0:2 * HG, 0:N], ACT.Copy).then_inc(s_mxT, 1)
                elif kind == "F2":
                    wait(s_misc, misc_no[e] + 1)
                    eng.activation(concT[:, :], misc[:, 0:N], ACT.Copy).then_inc(s_concT, 1)
            wait(s_var, 2)
            eng.activation(rstd[:, :], var[:, :], ACT.Sqrt).then_inc(s_sqrt, 1)
            for k in range(NBLK):
                wait(s_tr, k + 1)
                eng.activation(xn2T[:, k, :], misc[:, :], ACT.Copy).then_inc(s_trf, 1)
            wait(s_lg, 1)
            eng.activation(lg[:, :, :], lg[:, :, :], ACT.Exp).then_inc(s_pe, 1)
            hp = [st[0], st[1], st[2], mxp[0]]
            for i in range(NBLK * NE):
                ex = i % NE
                for c in range(HC):
                    wait(s_hp, HC * i + c + 1)
                    wait(s_y, i - 1)
                    eng.activation(hid[:, i % 2, c, :], hp[c][:, :], ACT.Gelu_apprx_tanh,
                                   bias=b1_sb[:, ex * HC + c:ex * HC + c + 1]).then_inc(s_hg, 1)

        @block.vector
        def _(eng):
            wait = waiter(eng)
            own = [0]

            def done(ins):
                ins.then_inc(s_dve, 1)
                own[0] += 1
                eng.wait_ge(s_dve, own[0])

            def statistics(i):
                done(eng.bn_stats(bst[:, i % 2, :], x_sb[:, i, :]))
                eng.bn_aggr(stat[:, i, :], bst[:, i % 2, :]).then_inc(s_dve, 1)
                own[0] += 1

            def inverse_deviation(nth):
                eng.wait_ge(s_dve, own[0])
                eng.tensor_scalar(var[:, :], stat[:, :, 1], LN_EPS, None, ALU.add)\
                   .then_inc(s_var, 1)
                wait(s_var, nth)
                wait(s_sqrt, nth)
                done(eng.reciprocal(rstd[:, :], rstd[:, :]))
                done(eng.tensor_tensor(tmp[:, :], rstd[:, :], rstd[:, :], ALU.mult))
                done(eng.tensor_tensor(tmp[:, :], tmp[:, :], var[:, :], ALU.mult))
                done(eng.tensor_scalar(tmp[:, :], tmp[:, :], -0.5, 1.5, ALU.mult, ALU.add))
                done(eng.tensor_tensor(rstd[:, :], rstd[:, :], tmp[:, :], ALU.mult))
                eng.scalar_tensor_tensor(nmr[:, :], stat[:, :, 0], -1.0, rstd[:, :],
                                         ALU.mult, ALU.mult).then_inc(s_rstd, 1)

            eng.memset(vaug, 1.0).then_inc(s_init, 1)
            for e in range(NE):
                eng.memset(rank[:, e:e + 1], float(NE - e)).then_inc(s_init, 1)
            for i in range(TILES):
                if i % (TILES // 4) == 0:
                    wait(s_x[i // (TILES // 4)], 16)
                statistics(i)
            inverse_deviation(1)

            n_mx = 0
            for e in events:
                kind = e[0]
                if kind == "MX":
                    G, m = e[1:]
                    tj, w = divmod(m, NW)
                    wait(s_mxp, n_mx + 1)
                    eng.tensor_reduce(mx[:, G % 2, tj, w:w + 1], mxp[n_mx % 2][:, 0:WIN],
                                      AX.X, ALU.max).then_inc(s_red, 1)
                    n_mx += 1
                elif kind == "MF":
                    G = e[1]
                    wait(s_red, n_mx)
                    if G > 0:
                        wait(s_misc, misc_no[("MT", G - 1)] + 1)
                    done(eng.tensor_reduce(nmx[:, :], mx[:, G % 2, :, :], AX.X, ALU.max,
                                           negate=True))
                    neg = nmx[:, :].rearrange("p (t j) -> p t j", t=NT)
                    done(eng.tensor_copy(mxhl[:, :, 0, :], neg))
                    eng.tensor_tensor(mxhl[:, :, 1, :], neg, mxhl[:, :, 0, :].bitcast(F32),
                                      ALU.subtract).then_inc(s_mxhl, 1)
                elif kind == "Q":
                    wait(s_qhi, e[1] + 1)
                    eng.tensor_tensor(qhl[:, 1, :], misc[:, 0:N], qhl[:, 0, :].bitcast(F32),
                                      ALU.subtract).then_inc(s_qlo, 1)
                elif kind == "K":
                    b, c = e[1:]
                    k0, kn = KCH[c]
                    wait(s_khi, len(KCH) * b + c + 1)
                    eng.tensor_tensor(khl[:, 1, k0:k0 + kn], misc[:, 0:kn],
                                      khl[:, 0, k0:k0 + kn].bitcast(F32),
                                      ALU.subtract).then_inc(s_klo, 1)
                elif kind == "F1":
                    wait(s_misc, misc_no[e] + 1)
                    fin = misc[:, 0:NT * H * VC].rearrange("p (h c) -> p h c", c=VC)
                    done(eng.reciprocal(rden[:, :], fin[:, :, DH]))
                    eng.tensor_tensor(conc[:, :, :, :].rearrange("p t h e -> p (t h) e"),
                                      fin[:, :, 0:DH],
                                      rden[:, :].unsqueeze(2).to_broadcast([P, NT * H, DH]),
                                      ALU.mult).then_inc(s_conc, 1)
                elif kind == "F3":
                    b = e[1]
                    wait(s_misc, misc_no[e] + 1)
                    wait(s_tanh, 1)
                    xb = x_sb[:, b * NT:(b + 1) * NT, :].rearrange("p t d -> p (t d)")
                    eng.scalar_tensor_tensor(xb, misc[:, 0:N], tgate[:, 0:1], xb,
                                             ALU.mult, ALU.add).then_inc(s_res, 1)
                    wait(s_res, b + 1)
                    for t in range(NT):
                        statistics(b * NT + t)

            inverse_deviation(2)
            wait(s_rt, 1)
            logits = mxp[1][:, 0:TILES * NE].rearrange("p (t e) -> p t e", e=NE)

            def per_tile(ap):
                return ap.unsqueeze(2).to_broadcast([P, TILES, NE])

            ranks = rank[:, :].unsqueeze(1).to_broadcast([P, TILES, NE])
            p1, p2, den = top[:, 0, :], top[:, 1, :], top[:, 2, :]
            done(eng.tensor_reduce(p1, logits, AX.X, ALU.max))
            eng.tensor_tensor(lg[:, :, :], logits, per_tile(p1), ALU.subtract).then_inc(s_lg, 1)
            wait(s_pe, 1)
            done(eng.tensor_reduce(den, lg[:, :, :], AX.X, ALU.add))
            done(eng.reciprocal(den, den))
            done(eng.tensor_tensor(lg[:, :, :], lg[:, :, :], per_tile(den), ALU.mult))
            wait(s_init, N_INIT)

            def first_of_largest(value, hot):
                done(eng.tensor_reduce(value, lg[:, :, :], AX.X, ALU.max))
                done(eng.tensor_tensor(eq[:, :, :], lg[:, :, :], per_tile(value), ALU.is_equal))
                done(eng.tensor_tensor(eq[:, :, :], eq[:, :, :], ranks, ALU.mult))
                done(eng.tensor_reduce(tmp[:, :], eq[:, :, :], AX.X, ALU.max))
                done(eng.tensor_tensor(hot, eq[:, :, :], per_tile(tmp[:, :]), ALU.is_equal))

            first_of_largest(p1, oh1[:, :, :])
            done(eng.scalar_tensor_tensor(lg[:, :, :], oh1[:, :, :], -2.0, lg[:, :, :],
                                          ALU.mult, ALU.add))
            first_of_largest(p2, cw[:, :, :])
            done(eng.scalar_tensor_tensor(den, p1, TOPK_EPS, p2, ALU.add, ALU.add))
            done(eng.reciprocal(den, den))
            done(eng.tensor_tensor(p1, p1, den, ALU.mult))
            done(eng.tensor_tensor(p2, p2, den, ALU.mult))
            done(eng.tensor_tensor(oh1[:, :, :], oh1[:, :, :], per_tile(p1), ALU.mult))
            done(eng.tensor_tensor(cw[:, :, :], cw[:, :, :], per_tile(p2), ALU.mult))
            done(eng.tensor_tensor(cw[:, :, :], cw[:, :, :], oh1[:, :, :], ALU.add))

            wait(s_ffw, 48)
            for i in range(NBLK * NE):
                k, ex = divmod(i, NE)
                for t in range(BT):
                    w = cw[:, k * BT + t, ex:ex + 1]
                    if ex == 0:
                        ins = eng.tensor_scalar(acc[:, t, :], b2_sb[:, ex, :], w, None, ALU.mult)
                    else:
                        wait(s_add, BT * (i - 1) + t + 1)
                        ins = eng.scalar_tensor_tensor(acc[:, t, :], b2_sb[:, ex, :], w,
                                                       acc[:, t, :], ALU.mult, ALU.add)
                    ins.then_inc(s_bias, 1)
                wait(s_y, i + 1)
                for t in range(BT):
                    w = cw[:, k * BT + t, ex:ex + 1]
                    wait(s_bias, BT * i + t + 1)
                    eng.scalar_tensor_tensor(acc[:, t, :], pv[i % 2][:, t * D:(t + 1) * D], w,
                                             acc[:, t, :], ALU.mult, ALU.add).then_inc(s_add, 1)
                if ex == NE - 1:
                    wait(s_add, BT * (i + 1))
                    xb = x_sb[:, k * BT:(k + 1) * BT, :].rearrange("p t d -> p (t d)")
                    eng.scalar_tensor_tensor(
                        xb, acc.rearrange("p t d -> p (t d)"), tgate[:, 1:2], xb,
                        ALU.mult, ALU.add).then_inc(s_o, 1)
                    wait(s_o, k + 1)


N_W = 9
N_INIT = 1 + NE

_INS = ["x", "ctxT", "gates", "wq", "wk", "wv", "woT", "rwT", "w1T", "b1T", "w2T", "b2", "ident",
        "sel"]


def _lay_out(i):
    sel = np.zeros((P, HG * VC), np.float32)
    for j in range(HG):
        for c in range(VC):
            sel[32 * j + c, j * VC + c] = 1.0
    a = {k: np.asarray(v) for k, v in i.items()}
    heads = lambda w: w.transpose(1, 0, 2).reshape(D, D)
    return {
        "x": a["x"].reshape(B * N, D),
        "ctxT": a["ctx_1024"].transpose(0, 2, 1),
        "gates": np.concatenate([a["g_xattn"], a["g_ffn"]]),
        "wq": heads(a["L0_xattn_Wq"]),
        "wk": heads(a["L0_xattn_Wk"]),
        "wv": heads(a["L0_xattn_Wv"]),
        "woT": a["L0_xattn_Wo"].T,
        "rwT": a["L0_ffn_router_w"].T,
        "w1T": a["L0_ffn_w1"].transpose(2, 0, 1).reshape(D, NE * HID),
        "b1T": a["L0_ffn_b1"].reshape(NE * HC, P).T,
        "w2T": a["L0_ffn_w2"].transpose(0, 2, 1).reshape(NE * HC, P, D).transpose(1, 0, 2),
        "b2": a["L0_ffn_b2"].reshape(NE * D),
        "ident": np.eye(P, dtype=np.float32),
        "sel": sel,
    }


def kernel(**inputs):
    import concourse.bacc as _bacc
    from concourse.bass_utils import run_bass_kernel_spmd as _run

    nc = _bacc.Bacc("TRN2", target_bir_lowering=False, num_devices=1)
    laid = _lay_out(inputs)
    arrays, args = {}, []
    for name in _INS:
        a = np.ascontiguousarray(laid[name])
        arrays[f"in_{name}"] = a
        args.append(nc.dram_tensor(f"in_{name}", a.shape, mybir.dt.from_np(a.dtype),
                                   kind="ExternalInput").ap())
    out = nc.dram_tensor("out_x", (B * N, D), F32, kind="ExternalOutput").ap()
    build(nc, *args, out)
    r = _run(nc, [arrays], core_ids=[0])
    return r.results[0]["out_x"].reshape(B, N, D)
```

```python
import math
from contextlib import ExitStack

import concourse.bass as bass
import numpy as np
from concourse import mybir

F32 = mybir.dt.float32
F32R = mybir.dt.float32r
I32 = mybir.dt.int32
ALU = mybir.AluOpType
ACT = mybir.ActivationFunctionType
AX = mybir.AxisListType

B, N, D = 16, 256, 128
M = 1601
H, DH = 16, 8
NE, HID = 8, 512
P = 128
SCALE = 0.125
LN_EPS = 1e-5
TOPK_EPS = 1e-8

NT = N // P
TILES = B * NT
HG = 4
NG = H // HG
KT = -(-M // P)
UNITS = NG * KT
WIN = 402
WSTART = [0, 400, 800, M - WIN]
NW = len(WSTART)
KCH = [(0, 401), (401, 400), (801, 400), (1201, 400)]
VCH = [(0, 4), (4, 4), (8, 4), (12, 1)]
VC = DH + 1
VW = VC * (H - 1) + 32
PARTS = 3
MAXROW = PARTS * HG * DH
SCORE_ROWS = MAXROW + 2
LAG = 3
AHEAD = KT + 5
ST_BUFS = 3
MX_BUFS = 3
PT_BUFS = 8
BLK = 512
NBLK = B * N // BLK
BT = BLK // P
HC = HID // P
CHUNKS = NBLK * NE * HC
RING = 4
HLAG = 3
CWB = 3
K_PART, Q_PART = (0, 1, 0), (0, 0, 1)
GUESS = float(0x5F3759DF)
NEWTON = 3


NEXT_AT = {0: ("N", "X"), 6: ("X",), 10: ("Q",), 14: ("K", 0), 16: ("K", 1), 18: ("K", 2),
           20: ("K", 3), 23: ("PK", 0), 28: ("V", 0), 29: ("PK", 1), 30: ("V", 1), 32: ("V", 2),
           34: ("V", 3), 37: ("PK", 2), 42: ("PK", 3)}
LAST_AT = {4: ("F1", 1), 8: ("F2",), 12: ("F3",), 14: ("N", "L"), 24: ("L",), 26: ("R",)}
HALF_AT, TURN_AT = 44, 9


def key_rows(kt):
    return min(P, M - kt * P)


def schedule():
    ev = []
    n_max = HG * NT * NW
    n_groups = B * NG

    def at_batch(e, b):
        return e + (b,) if e[0] == "N" else e[:1] + (b,) + e[1:]

    def last(v):
        return v % KT == KT - 1

    def maxima(v):
        windows = []
        for G, kt in (divmod(v, KT), divmod(v + 1, KT)):
            if G < n_groups:
                windows += [[("MX", G, m)] for m in range(kt * n_max // KT, (kt + 1) * n_max // KT)]
                if kt == KT - 1:
                    windows[-1].append(("MF", G))
        parts = [[] for _ in range(5)]
        for i, w in enumerate(windows):
            parts[i * 5 // len(windows)] += w
        return parts

    ev += [("N", "X", 0)] + [("K", 0, c) for c in range(len(KCH))] + [("X", 0), ("Q", 0)]
    ev += [("PK", 0, 0), ("PK", 0, 1)]
    ev += [("V", 0, c) for c in range(len(VCH))]
    for v in range(0, AHEAD, 2):
        ev += sum(maxima(v), [])
        if v == KT + 1:
            ev += [("MT", 0), ("PK", 0, 2), ("PK", 0, 3)]
    for u in range(B * UNITS):
        b, r = divmod(u, UNITS)
        G = u // KT
        if u % 2 == 0:
            parts = maxima(u + AHEAD)
        copy = [("PC", (u - LAG) // KT)] if u >= LAG and last(u - LAG) else []
        ev += copy * (u % 2) + [("S", u, 0)] + parts.pop(0)
        ev += [("S", u, 1)] + copy * (1 - u % 2) + parts.pop(0)
        if u % 2 and u >= LAG:
            ev += [("PV", v) for v in (u - LAG, u - LAG + 1) if v % 2 or not last(v)]
        elif u % 2 == 0 and u >= LAG and last(u - LAG + 1):
            ev.append(("PV", u - LAG + 1))
        if u % 2:
            ev += parts.pop(0)
        if u % KT == TURN_AT and G + 1 < n_groups:
            ev.append(("MT", G + 1))
        if b + 1 < B and r in NEXT_AT:
            ev.append(at_batch(NEXT_AT[r], b + 1))
        if b > 0 and r in LAST_AT:
            ev.append(at_batch(LAST_AT[r], b - 1))
        if r == HALF_AT:
            ev.append(("F1", b, 0))
    b = B - 1
    ev += [("PV", B * UNITS - n) for n in range(LAG - 1, 0, -1)] + [("PC", n_groups - 1)]
    ev += [at_batch(LAST_AT[r], b) for r in sorted(LAST_AT)]
    return ev


MISC = ("X", "Q", "K", "V", "MT", "F1", "F2", "F3", "L", "R")


def build(nc, x, ctxT, gates, wq, wk, wv, woT, rwT, w1T, b1T, w2T, b2T, ident, ehots, out):
    events = schedule()
    misc_no = {}
    for e in events:
        if e[0] in MISC:
            misc_no[e] = len(misc_no)
    norms = [e[1:] for e in events if e[0] == "N"]
    norm_no = {e: i for i, e in enumerate(norms)}

    ctx = ExitStack()
    with ctx:
        def sb(name, shape, dt=F32):
            return ctx.enter_context(nc.sbuf_tensor(name, shape, dt))

        def sem(name):
            return ctx.enter_context(nc.semaphore(name))

        def carve(flat, sizes):
            at, parts = 0, []
            for n in sizes:
                parts.append(flat[:, at:at + n])
                at += n
            return parts

        x_sb = sb("x_sb", [P, TILES, D])
        xn2T = sb("xn2T", [P, B * N])
        kpack = sb("kpack", [P, 2, NG, M], F32R)
        khl = sb("khl", [P, 2, M], F32R)
        qmask = sb("qmask", [P, 2, NG, HG, N], F32R)
        qhl = sb("qhl", [P, 2, N], F32R)
        arena = sb("arena", [P, 2 * M + 2 * KT * VW + PT_BUFS * BLK])
        ctx_f, vaug_f, pt_f = carve(arena, [2 * M, 2 * KT * VW, PT_BUFS * BLK])
        ctx_sb = ctx_f.rearrange("p (k m) -> p k m", k=2)
        vaug = vaug_f.rearrange("p (k t w) -> p k t w", k=2, t=KT)
        pt = pt_f.rearrange("p (k n) -> p k n", k=PT_BUFS)
        hf, cwb, yt, acc, eq_f, oh_f = carve(
            arena, [RING * BLK, CWB * BLK, 2 * BLK, 2 * BLK, TILES * NE, TILES * NE])
        hf, cwb, yt, acc = (v.rearrange("p (k n) -> p k n", n=BLK) for v in (hf, cwb, yt, acc))
        eq, oh1 = (v.rearrange("p (t e) -> p t e", e=NE) for v in (eq_f, oh_f))
        w1h, w1l, w2h, cwhl_f = carve(kpack[:, :, :, :].rearrange("p a g m -> p (a g m)"),
                                      [NE * HID] * 3 + [TILES * 2 * NE])
        cwhl = cwhl_f.rearrange("p (t s e) -> p t s e", s=2, e=NE)
        w2l, hh, hl = carve(qmask[:, :, :, :, :].rearrange("p a g j n -> p (a g j n)"),
                            [NE * HID, RING * BLK, RING * BLK])
        hh, hl = (v.rearrange("p (k n) -> p k n", n=BLK) for v in (hh, hl))
        xh, xl, cwT = carve(khl[:, :, :].rearrange("p s m -> p (s m)"), [2 * BLK] * 3)
        xh, xl, cwT = (v.rearrange("p (k n) -> p k n", n=BLK) for v in (xh, xl, cwT))

        wq_sb, wk_sb, wv_sb, wo_sb = (sb(n, [P, D]) for n in ("wq_sb", "wk_sb", "wv_sb", "wo_sb"))
        id_sb = sb("id_sb", [P, P])
        rw_sb = sb("rw_sb", [P, NE])
        wraw = sb("wraw", [P, 2, 2, HID])
        b1_sb = sb("b1_sb", [P, NE * HC])
        b2_sb = sb("b2_sb", [P, NE])
        gate = sb("gate", [P, 2])
        tgate = sb("tgate", [P, 2])
        xn = sb("xn", [P, NT, D])
        xnT = sb("xnT", [P, N])
        pv_sb = sb("pv_sb", [P, 2, BLK])
        conc = sb("conc", [P, NT, NG, HG, DH])
        concT = sb("concT", [P, N])
        rden = sb("rden", [P, NT * H // 2])
        mx = sb("mx", [P, NT * HG, NW])
        nmx = sb("nmx", [P, NT * HG])
        mxhl = sb("mxhl", [P, NT, 2, HG], F32R)
        mxT = sb("mxT", [2 * HG, N], F32R)
        bst = sb("bst", [P, NT, 6])
        stat = sb("stat", [P, NT, 2])
        var = sb("var", [P, NT])
        half = sb("half", [P, NT], I32)
        rstd = sb("rstd", [P, NT])
        tmp = sb("tmp", [P, NT])
        lg = sb("lg", [P, TILES, NE])
        cw = sb("cw", [P, TILES, NE])
        top = sb("top", [P, 4, TILES])
        rank = sb("rank", [P, NE])
        ehot_f = sb("ehot_f", [2 * NE, NE])
        ehot = sb("ehot", [2 * NE, NE, P], F32R)

        bank = [ctx.enter_context(nc.psum_tensor(f"bank{i}", [P, BLK], F32)) for i in range(8)]
        st, mxp, pv, misc = bank[0:ST_BUFS], bank[3:3 + MX_BUFS], bank[6], bank[7]
        hp, turn, yp, spread = bank[0:RING], bank[4], bank[5:7], misc

        s_w = sem("s_w")
        s_w2 = sem("s_w2")
        s_x0 = sem("s_x0")
        s_x = sem("s_x")
        s_ctx = [sem("s_ctx0"), sem("s_ctx1")]
        s_wraw = [sem("s_wraw0"), sem("s_wraw1")]
        s_fill = sem("s_fill")
        s_init = sem("s_init")
        s_seed = sem("s_seed")
        s_pool = sem("s_pool")
        s_tanh = sem("s_tanh")
        s_xn = sem("s_xn")
        s_misc = sem("s_misc")
        s_xnT = sem("s_xnT")
        s_qhi = sem("s_qhi")
        s_qlo = sem("s_qlo")
        s_khi = sem("s_khi")
        s_klo = sem("s_klo")
        s_qd = [[sem(f"s_qd{i}{g}") for g in range(NG)] for i in range(2)]
        s_kd = [[sem(f"s_kd{i}{g}") for g in range(NG)] for i in range(2)]
        s_v = sem("s_v")
        s_mxp = sem("s_mxp")
        s_red = sem("s_red")
        s_mxhl = sem("s_mxhl")
        s_mxT = sem("s_mxT")
        s_mxd = [sem("s_mxd0"), sem("s_mxd1")]
        s_st = sem("s_st")
        s_exp = sem("s_exp")
        s_pv = sem("s_pv")
        s_pvs = sem("s_pvs")
        s_conc = sem("s_conc")
        s_concT = sem("s_concT")
        s_dve = sem("s_dve")
        s_res = sem("s_res")
        s_x2T = sem("s_x2T")
        s_lgt = sem("s_lgt")
        s_lg = sem("s_lg")
        s_pe = sem("s_pe")
        s_cw = sem("s_cw")
        s_wh = sem("s_wh")
        s_wl = sem("s_wl")
        s_xh = sem("s_xh")
        s_xl = sem("s_xl")
        s_hp = sem("s_hp")
        s_hg = sem("s_hg")
        s_hh = sem("s_hh")
        s_hl = sem("s_hl")
        s_f2 = sem("s_f2")
        s_cwp = sem("s_cwp")
        s_cwT = sem("s_cwT")
        s_cbp = sem("s_cbp")
        s_cb = sem("s_cb")
        s_yt = sem("s_yt")
        s_acc = sem("s_acc")
        s_tp = sem("s_tp")
        s_o = sem("s_o")
        s_out = sem("s_out")

        signal = {"X": s_xnT, "Q": s_qlo, "K": s_klo, "V": s_v, "MT": s_mxT, "F1": s_conc,
                  "F2": s_concT, "F3": s_res, "L": s_x2T, "R": s_lgt}
        uses = dict.fromkeys(signal, 0)
        read_out = []
        for e in misc_no:
            uses[e[0]] += 1
            read_out.append((signal[e[0]], uses[e[0]]))

        block = ctx.enter_context(nc.Block())

        def waiter(eng):
            seen = {}

            def wait(s, value):
                if value > seen.get(id(s), 0):
                    seen[id(s)] = value
                    eng.wait_ge(s, value)
            return wait

        @block.sync
        def _(eng):
            wait = waiter(eng)
            xs = x.rearrange("(t p) d -> p t d", p=P)
            eng.dma_start(x_sb[:, 0:NT, :], xs[:, 0:NT, :]).then_inc(s_x0, 16)
            eng.dma_start(wk_sb[:, :], wk).then_inc(s_w, 16)
            eng.dma_start(ctx_sb[:, 0, :], ctxT[0]).then_inc(s_ctx[0], 16)
            for dst, src in ((id_sb, ident), (wq_sb, wq), (wv_sb, wv)):
                eng.dma_start(dst[:, :], src).then_inc(s_w, 16)
            eng.dma_start(x_sb[:, NT:TILES, :], xs[:, NT:TILES, :]).then_inc(s_x, 16)
            for dst, src in ((wo_sb, woT), (rw_sb, rwT), (b1_sb, b1T), (b2_sb, b2T),
                             (gate, gates.partition_broadcast(P)), (ehot_f, ehots)):
                eng.dma_start(dst[:, :], src).then_inc(s_w2, 16)
            eng.dma_start(ctx_sb[:, 1, :], ctxT[1]).then_inc(s_ctx[1], 16)

            def load_expert(ex):
                for i, w in enumerate((w1T, w2T)):
                    eng.dma_start(wraw[:, ex % 2, i, :], w[:, ex * HID:(ex + 1) * HID]
                                  ).then_inc(s_wraw[ex % 2], 16)

            for e in events:
                if e[0] == "PK":
                    b, g = e[1:]
                    if b == 0:
                        wait(s_fill, 2)
                    wait(s_qlo, b + 1)
                    wait(s_klo, len(KCH) * (b + 1))
                    wait(s_st, 2 * UNITS * (b - 1))
                    for part in range(PARTS):
                        r = part * HG * DH
                        eng.dma_start(kpack[r:r + HG * DH, b % 2, g, :].bitcast(F32),
                                      khl[g * HG * DH:(g + 1) * HG * DH, K_PART[part], :]
                                      .bitcast(F32)).then_inc(s_kd[b % 2][g], 16)
                        for j in range(HG):
                            h, rj = g * HG + j, r + j * DH
                            eng.dma_start(qmask[rj:rj + DH, b % 2, g, j, :].bitcast(F32),
                                          qhl[h * DH:(h + 1) * DH, Q_PART[part], :]
                                          .bitcast(F32)).then_inc(s_qd[b % 2][g], 16)
                elif e[0] == "V" and e[2] == len(VCH) - 1:
                    b = e[1]
                    if b + 2 < B:
                        wait(s_v, len(VCH) * (b + 1))
                        eng.dma_start(ctx_sb[:, b % 2, :], ctxT[b + 2]).then_inc(s_ctx[b % 2], 16)
                    if b == 0:
                        load_expert(0)
                        load_expert(1)
                elif e[0] == "MT":
                    b, g = divmod(e[1], NG)
                    wait(s_mxT, e[1] + 1)
                    for half_no in range(2):
                        eng.dma_start(
                            qmask[MAXROW + half_no:MAXROW + half_no + 1, b % 2, g, :, :]
                            .bitcast(F32),
                            mxT[half_no * HG:(half_no + 1) * HG, :].bitcast(F32)
                        ).then_inc(s_mxd[e[1] % 2], 16)
            for ex in range(2, NE):
                wait(s_wh, ex - 1)
                wait(s_wl, ex - 1)
                load_expert(ex)
            outs = out.rearrange("(t p) d -> p t d", p=P)
            for k in range(NBLK):
                wait(s_o, k + 1)
                eng.dma_start(outs[:, k * BT:(k + 1) * BT, :],
                              x_sb[:, k * BT:(k + 1) * BT, :]).then_inc(s_out, 16)
            eng.wait_ge(s_out, 16 * NBLK)

        @block.gpsimd
        def _(eng):
            wait = waiter(eng)
            own = [0]

            def done(ins):
                ins.then_inc(s_pool, 1)
                own[0] += 1
                eng.wait_ge(s_pool, own[0])

            eng.memset(kpack[MAXROW:P, :, :, :].bitcast(F32), 1.0).then_inc(s_fill, 1)
            wait(s_fill, 1)
            eng.memset(qmask[:, :, :, :, :].bitcast(F32), 0.0).then_inc(s_fill, 1)
            wait(s_fill, 2)
            for e in events:
                if e[0] != "N":
                    continue
                _, which, b = e
                i = norm_no[which, b]
                wait(s_seed, i + 1)
                for _ in range(NEWTON):
                    done(eng.tensor_tensor(tmp[:, :], rstd[:, :], rstd[:, :], ALU.mult))
                    done(eng.tensor_tensor(tmp[:, :], tmp[:, :], var[:, :], ALU.mult))
                    done(eng.tensor_scalar(tmp[:, :], tmp[:, :], -0.5, 1.5, ALU.mult, ALU.add))
                    done(eng.tensor_tensor(rstd[:, :], rstd[:, :], tmp[:, :], ALU.mult))
                if i > 0:
                    wait(s_misc, misc_no[norms[i - 1]] + 1)
                for t in range(NT):
                    eng.tensor_scalar(xn[:, t, :], x_sb[:, b * NT + t, :], stat[:, t, 0:1],
                                      rstd[:, t:t + 1], ALU.subtract, ALU.mult).then_inc(s_xn, 1)
            n = 0
            for i in range(NBLK * NE):
                k, ex = divmod(i, NE)
                wait(s_yt, i + 1)
                if ex > 0:
                    wait(s_acc, n)
                    eng.tensor_tensor(acc[:, k % 2, :], acc[:, k % 2, :], yt[:, i % 2, :],
                                      ALU.add).then_inc(s_acc, 1)
                    n += 1

        @block.tensor
        def _(eng):
            wait = waiter(eng)

            def misc_bank(e):
                if misc_no[e]:
                    wait(*read_out[misc_no[e] - 1])

            n_mx = 0
            wait(s_w, 16 * N_W)
            for e in events:
                kind = e[0]
                if kind == "S":
                    u, p = e[1:]
                    b, r = divmod(u, UNITS)
                    g, kt = divmod(r, KT)
                    G, c, n = b * NG + g, 2 * u + p, key_rows(kt)
                    wait(s_mxd[G % 2], 32 * (G // 2 + 1))
                    wait(s_exp, c - ST_BUFS + 1)
                    eng.matmul(st[c % ST_BUFS][0:n, :],
                               kpack[0:SCORE_ROWS, b % 2, g, kt * P:kt * P + n],
                               qmask[0:SCORE_ROWS, b % 2, g, 2 * p:2 * p + 2, :],
                               start=True, stop=True).then_inc(s_st, 1)
                elif kind == "MX":
                    G, m = e[1:]
                    b, g = divmod(G, NG)
                    tj, w = divmod(m, NW)
                    t, j = divmod(tj, HG)
                    if m == 0:
                        wait(s_qd[b % 2][g], 16 * PARTS * HG * (b // 2 + 1))
                        wait(s_kd[b % 2][g], 16 * PARTS * (b // 2 + 1))
                    wait(s_red, n_mx - MX_BUFS + 1)
                    eng.matmul(mxp[n_mx % MX_BUFS][:, 0:WIN],
                               qmask[0:MAXROW, b % 2, g, j, t * P:(t + 1) * P],
                               kpack[0:MAXROW, b % 2, g, WSTART[w]:WSTART[w] + WIN],
                               start=True, stop=True).then_inc(s_mxp, 1)
                    n_mx += 1
                elif kind == "MT":
                    misc_bank(e)
                    wait(s_mxhl, e[1] + 1)
                    for t in range(NT):
                        ins = eng.transpose(
                            misc[0:2 * HG, t * P:(t + 1) * P],
                            mxhl[:, t, :, :].rearrange("p s j -> p (s j)").bitcast(F32), id_sb[:, :])
                    ins.then_inc(s_misc, 1)
                elif kind == "PV":
                    u = e[1]
                    b, r = divmod(u, UNITS)
                    g, kt = divmod(r, KT)
                    n = key_rows(kt)
                    wait(s_v, len(VCH) * (b + 1))
                    wait(s_pvs, b * NG + g)
                    for j in range(HG):
                        if j % 2 == 0:
                            wait(s_exp, 2 * u + j // 2 + 1)
                        h = g * HG + j
                        ins = eng.matmul(
                            pv[32 * j:32 * j + 32, (g % 2) * N:(g % 2 + 1) * N],
                            vaug[0:n, b % 2, kt, VC * h:VC * h + 32],
                            pt[0:n, (2 * u + j // 2) % PT_BUFS, (j % 2) * N:(j % 2 + 1) * N],
                            start=(kt == 0), stop=(kt == KT - 1), tile_position=(0, 32 * j))
                    ins.then_inc(s_pv, 1)
                elif kind in ("X", "L"):
                    misc_bank(e)
                    wait(s_xn, NT * (norm_no[e] + 1))
                    for t in range(NT):
                        ins = eng.transpose(misc[:, t * P:(t + 1) * P], xn[:, t, :], id_sb[:, :])
                    ins.then_inc(s_misc, 1)
                elif kind == "Q":
                    misc_bank(e)
                    wait(s_xnT, e[1] + 1)
                    eng.matmul(misc[:, 0:N], wq_sb[:, :], xnT[:, :],
                               start=True, stop=True).then_inc(s_misc, 1)
                elif kind == "K":
                    b, c = e[1:]
                    k0, kn = KCH[c]
                    misc_bank(e)
                    wait(s_ctx[b % 2], 16 * (b // 2 + 1))
                    eng.matmul(misc[:, 0:kn], wk_sb[:, :], ctx_sb[:, b % 2, k0:k0 + kn],
                               start=True, stop=True).then_inc(s_misc, 1)
                elif kind == "V":
                    b, c = e[1:]
                    misc_bank(e)
                    t0, tn = VCH[c]
                    for i in range(tn):
                        n = key_rows(t0 + i)
                        ins = eng.matmul(misc[0:n, i * D:(i + 1) * D],
                                         ctx_sb[:, b % 2, (t0 + i) * P:(t0 + i) * P + n],
                                         wv_sb[:, :], start=True, stop=True)
                    ins.then_inc(s_misc, 1)
                elif kind == "F1":
                    b, i = e[1:]
                    misc_bank(e)
                    wait(s_pvs, b * NG + 2 * i + 2)
                    for q in range(2 * NT):
                        at = q % NT * 2 + q // NT
                        ins = eng.transpose(misc[:, at * P:(at + 1) * P],
                                            pv_sb[:, i, q * P:(q + 1) * P], id_sb[:, :])
                    ins.then_inc(s_misc, 1)
                elif kind == "F2":
                    misc_bank(e)
                    wait(s_conc, 2 * (e[1] + 1))
                    for t in range(NT):
                        ins = eng.transpose(misc[:, t * P:(t + 1) * P],
                                            conc[:, t, :, :, :].rearrange("p g j e -> p (g j e)"),
                                            id_sb[:, :])
                    ins.then_inc(s_misc, 1)
                elif kind == "R":
                    b = e[1]
                    misc_bank(e)
                    wait(s_x2T, b + 1)
                    for t in range(NT):
                        i = b * NT + t
                        ins = eng.matmul(misc[:, t * NE:(t + 1) * NE], xn2T[:, i * P:(i + 1) * P],
                                         rw_sb[:, :], start=True, stop=True)
                    ins.then_inc(s_misc, 1)
                elif kind == "F3":
                    misc_bank(e)
                    wait(s_concT, e[1] + 1)
                    wait(s_w2, 16 * N_W2)
                    for t in range(NT):
                        ins = eng.matmul(misc[:, t * P:(t + 1) * P], concT[:, t * P:(t + 1) * P],
                                         wo_sb[:, :], start=True, stop=True)
                    ins.then_inc(s_misc, 1)

            wait(s_exp, 2 * B * UNITS)
            wait(s_red, n_mx)
            wait(s_pvs, B * NG)
            wait(*read_out[-1])

            def weight_rows(k):
                wait(s_cw, 1)
                wait(s_o, k - 1)
                wait(s_cwT, k)
                for t in range(BT):
                    ins = eng.transpose(
                        turn[0:2 * NE, t * P:(t + 1) * P],
                        cwhl[:, k * BT + t, :, :].rearrange("p s e -> p (s e)").bitcast(F32),
                        id_sb[:, :])
                ins.then_inc(s_cwp, 1)

            def spread_weights(i):
                k, ex = divmod(i, NE)
                wait(s_cwT, k + 1)
                wait(s_cb, i)
                eng.matmul(spread[:, :], ehot[:, ex, :], cwT[0:2 * NE, k % 2, :],
                           start=True, stop=True).then_inc(s_cbp, 1)

            def turn_back(k):
                wait(s_acc, (NE - 1) * (k + 1))
                wait(s_cwT, min(k + 2, NBLK))
                for t in range(BT):
                    ins = eng.transpose(turn[:, t * P:(t + 1) * P],
                                        acc[:, k % 2, t * P:(t + 1) * P], id_sb[:, :])
                ins.then_inc(s_tp, 1)

            for q in range(CHUNKS + HLAG + 2 * HC):
                i, c = divmod(q, HC)
                if q < CHUNKS:
                    k, ex = divmod(i, NE)
                    w = slice((ex * HC + c) * P, (ex * HC + c + 1) * P)
                    if k == 0 and c == 0:
                        wait(s_wh, ex + 1)
                        wait(s_wl, ex + 1)
                    wait(s_xh, k + 1)
                    wait(s_xl, k + 1)
                    wait(s_hg, q - RING + 1)
                    pairs = ((w1h, xh), (w1h, xl), (w1l, xh))
                    for n, (lhs, rhs) in enumerate(pairs):
                        ins = eng.matmul(hp[q % RING][:, :], lhs[:, w], rhs[:, k % 2, :],
                                         start=(n == 0), stop=(n == 2))
                    ins.then_inc(s_hp, 1)
                f = q - HLAG
                if 0 <= f < CHUNKS:
                    i2, c2 = divmod(f, HC)
                    w = slice(((i2 % NE) * HC + c2) * P, ((i2 % NE) * HC + c2 + 1) * P)
                    wait(s_hl, f + 1)
                    if c2 == 0:
                        wait(s_yt, i2 - 1)
                    for n, (lhs, rhs) in enumerate(((w2h, hh), (w2h, hl), (w2l, hh))):
                        ins = eng.matmul(yp[i2 % 2][:, :], lhs[:, w], rhs[:, f % RING, :],
                                         start=(c2 == 0 and n == 0),
                                         stop=(c2 == HC - 1 and n == 2))
                    ins.then_inc(s_f2, 1)
                i3, c3 = divmod(q - 2 * HC + 1, HC)
                if c3 == 0 and 0 <= i3 < NBLK * NE:
                    if i3 == 0:
                        weight_rows(0)
                    spread_weights(i3)
                if c3 == 2 and i3 >= 0:
                    k3, e3 = divmod(i3, NE)
                    if e3 == 5 and k3 + 1 < NBLK:
                        weight_rows(k3 + 1)
                    if e3 == 1 and k3 > 0:
                        turn_back(k3 - 1)
            turn_back(NBLK - 1)

        @block.scalar
        def _(eng):
            wait = waiter(eng)
            for e in events:
                kind = e[0]
                if kind == "S":
                    u, p = e[1:]
                    c, n = 2 * u + p, key_rows(u % KT)
                    wait(s_st, c + 1)
                    wait(s_pv, (c - PT_BUFS) // 2 + 1)
                    eng.activation(pt[0:n, c % PT_BUFS, :], st[c % ST_BUFS][0:n, :], ACT.Exp,
                                   scale=SCALE).then_inc(s_exp, 1)
                elif kind == "PC":
                    b, g = divmod(e[1], NG)
                    wait(s_pv, KT * (e[1] + 1))
                    if b > 0:
                        wait(s_misc, misc_no["F1", b - 1, g // 2] + 1)
                    cols = slice(g % 2 * N, (g % 2 + 1) * N)
                    eng.activation(pv_sb[:, g // 2, cols], pv[:, cols], ACT.Copy).then_inc(s_pvs, 1)
                elif kind == "X":
                    wait(s_misc, misc_no[e] + 1)
                    eng.activation(xnT[:, :], misc[:, 0:N], ACT.Copy).then_inc(s_xnT, 1)
                elif kind == "L":
                    wait(s_misc, misc_no[e] + 1)
                    eng.activation(xn2T[:, e[1] * N:(e[1] + 1) * N], misc[:, 0:N],
                                   ACT.Copy).then_inc(s_x2T, 1)
                elif kind == "Q":
                    b = e[1]
                    wait(s_misc, misc_no[e] + 1)
                    if b > 0:
                        for g in range(NG):
                            wait(s_qd[(b - 1) % 2][g], 16 * PARTS * HG * ((b - 1) // 2 + 1))
                    eng.activation(qhl[:, 0, :], misc[:, 0:N], ACT.Copy).then_inc(s_qhi, 1)
                elif kind == "K":
                    b, c = e[1:]
                    k0, kn = KCH[c]
                    wait(s_misc, misc_no[e] + 1)
                    if b > 0 and c == 0:
                        for g in range(NG):
                            wait(s_kd[(b - 1) % 2][g], 16 * PARTS * ((b - 1) // 2 + 1))
                    eng.activation(khl[:, 0, k0:k0 + kn], misc[:, 0:kn], ACT.Copy).then_inc(s_khi, 1)
                elif kind == "V":
                    b, c = e[1:]
                    t0, tn = VCH[c]
                    n = key_rows(t0 + tn - 1)
                    wait(s_misc, misc_no[e] + 1)
                    wait(s_pv, UNITS * (b - 1))
                    if b == 0:
                        wait(s_init, N_INIT)
                    eng.activation(
                        vaug[0:n, b % 2, t0:t0 + tn, 0:VC * H]
                        .rearrange("p t (h c) -> p t h c", c=VC)[:, :, :, 0:DH],
                        misc[0:n, 0:tn * D].rearrange("p (t h e) -> p t h e", t=tn, e=DH),
                        ACT.Copy).then_inc(s_v, 1)
                elif kind == "MT":
                    G = e[1]
                    wait(s_misc, misc_no[e] + 1)
                    if G > 0:
                        wait(s_mxd[(G - 1) % 2], 32 * ((G - 1) // 2 + 1))
                    eng.activation(mxT[:, :], misc[0:2 * HG, 0:N], ACT.Copy).then_inc(s_mxT, 1)
                elif kind == "F2":
                    wait(s_misc, misc_no[e] + 1)
                    eng.activation(concT[:, :], misc[:, 0:N], ACT.Copy).then_inc(s_concT, 1)
                elif kind == "N" and e[1:] == ("X", 1):
                    wait(s_w2, 16 * N_W2)
                    eng.activation(tgate[:, :], gate[:, :], ACT.Tanh).then_inc(s_tanh, 1)
            def split_block(k):
                wait(s_hp, HC * NE * (k - 1))
                eng.activation(xh[:, k % 2, :], xn2T[:, k * BLK:(k + 1) * BLK],
                               ACT.Copy).then_inc(s_xh, 1)

            def split_weights(ex):
                w = slice(ex * HID, (ex + 1) * HID)
                wait(s_wraw[ex % 2], 32 * (ex // 2 + 1))
                eng.activation(w1h[:, w], wraw[:, ex % 2, 0, :], ACT.Copy)
                eng.activation(w2h[:, w], wraw[:, ex % 2, 1, :], ACT.Copy).then_inc(s_wh, 1)

            wait(s_pv, B * UNITS)
            split_weights(0)
            split_block(0)
            wait(s_lg, 1)
            eng.activation(lg[:, :, :], lg[:, :, :], ACT.Exp).then_inc(s_pe, 1)
            for q in range(CHUNKS + 2 * HC):
                i, c = divmod(q, HC)
                k, ex = divmod(i, NE)
                if q < CHUNKS:
                    wait(s_hp, q + 1)
                    wait(s_hl, q - RING + 1)
                    eng.activation(hf[:, q % RING, :], hp[q % RING][:, :], ACT.Gelu_apprx_tanh,
                                   bias=b1_sb[:, ex * HC + c:ex * HC + c + 1]).then_inc(s_hg, 1)
                    if q % 2 == 0:
                        wait(s_hg, q + 1)
                        wait(s_f2, q - RING + 1)
                        eng.activation(hh[:, q % RING, :], hf[:, q % RING, :],
                                       ACT.Copy).then_inc(s_hh, 1)
                    if c == 0 and k == 0 and ex + 1 < NE:
                        split_weights(ex + 1)
                    if c == 1 and ex == NE - 1 and k + 1 < NBLK:
                        split_block(k + 1)
                i3, c3 = divmod(q - 2 * HC + 1, HC)
                if c3 == 0 and 0 <= i3 < NBLK * NE:
                    if i3 == 0:
                        wait(s_cwp, 1)
                        eng.activation(cwT[0:2 * NE, 0, :], turn[0:2 * NE, :],
                                       ACT.Copy).then_inc(s_cwT, 1)
                    wait(s_cbp, i3 + 1)
                    wait(s_yt, i3 - CWB + 1)
                    eng.activation(cwb[:, i3 % CWB, :], spread[:, :], ACT.Copy).then_inc(s_cb, 1)
                if c3 == 2 and i3 >= 0:
                    k3, e3 = divmod(i3, NE)
                    if e3 == 5 and k3 + 1 < NBLK:
                        wait(s_cwp, k3 + 2)
                        wait(s_cbp, NE * k3)
                        eng.activation(cwT[0:2 * NE, (k3 + 1) % 2, :], turn[0:2 * NE, :],
                                       ACT.Copy).then_inc(s_cwT, 1)

        @block.vector
        def _(eng):
            wait = waiter(eng)
            own = [0]

            def done(ins):
                ins.then_inc(s_dve, 1)
                own[0] += 1
                eng.wait_ge(s_dve, own[0])

            def added(i):
                return 0 if i < 0 else (i // NE) * (NE - 1) + i % NE

            def add_to_x(eng, wait, k):
                wait(s_tp, k + 1)
                xb = x_sb[:, k * BT:(k + 1) * BT, :].rearrange("p t d -> p (t d)")
                eng.scalar_tensor_tensor(xb, turn[:, :], tgate[:, 1:2], xb,
                                         ALU.mult, ALU.add).then_inc(s_o, 1)

            eng.memset(vaug, 1.0).then_inc(s_init, 1)
            for e in range(NE):
                eng.memset(rank[:, e:e + 1], float(NE - e)).then_inc(s_init, 1)

            def after_own(ins):
                ins.then_inc(s_dve, 1)
                own[0] += 1

            def own_steps():
                eng.wait_ge(s_dve, own[0])

            chains = []

            def advance():
                if chains and next(chains[0], "over") == "over":
                    chains.pop(0)

            def finish_chains():
                while chains:
                    advance()

            def split_maxima():
                own_steps()
                neg = nmx[:, :].rearrange("p (t j) -> p t j", t=NT)
                after_own(eng.tensor_copy(mxhl[:, :, 0, :], neg))
                yield
                own_steps()
                eng.tensor_tensor(mxhl[:, :, 1, :], neg, mxhl[:, :, 0, :].bitcast(F32),
                                  ALU.subtract).then_inc(s_mxhl, 1)
                yield

            def norm_steps(which, b):
                if which == "X":
                    wait(s_x if b else s_x0, 16)
                else:
                    wait(s_res, b + 1)
                wait(s_xn, NT * norm_no[which, b])
                for t in range(NT):
                    after_own(eng.bn_stats(bst[:, t, :], x_sb[:, b * NT + t, :]))
                yield
                own_steps()
                for t in range(NT):
                    after_own(eng.bn_aggr(stat[:, t, :], bst[:, t, :]))
                yield
                own_steps()
                after_own(eng.tensor_scalar(var[:, :], stat[:, :, 1], LN_EPS, None, ALU.add))
                yield
                own_steps()
                after_own(eng.tensor_scalar(half[:, :], var[:, :].bitcast(I32), 1, None,
                                            ALU.logical_shift_right))
                yield
                own_steps()
                eng.tensor_scalar(rstd[:, :].bitcast(I32), half[:, :], -1.0, GUESS,
                                  ALU.mult, ALU.add).then_inc(s_seed, 1)
                yield

            n_mx = 0
            for e in events:
                kind = e[0]
                if kind in ("MT", "X", "L"):
                    finish_chains()
                if kind == "MX":
                    G, m = e[1:]
                    tj, w = divmod(m, NW)
                    wait(s_mxp, n_mx + 1)
                    if m == 0:
                        own_steps()
                    eng.tensor_reduce(mx[:, tj, w:w + 1], mxp[n_mx % MX_BUFS][:, 0:WIN],
                                      AX.X, ALU.max).then_inc(s_red, 1)
                    n_mx += 1
                    advance()
                elif kind == "MF":
                    G = e[1]
                    finish_chains()
                    wait(s_red, n_mx)
                    if G > 0:
                        wait(s_misc, misc_no[("MT", G - 1)] + 1)
                    after_own(eng.tensor_reduce(nmx[:, :], mx[:, :, :], AX.X, ALU.max,
                                                negate=True))
                    chains.append(split_maxima())
                elif kind == "N":
                    finish_chains()
                    chains.append(norm_steps(*e[1:]))
                elif kind == "Q":
                    wait(s_qhi, e[1] + 1)
                    eng.tensor_tensor(qhl[:, 1, :], misc[:, 0:N], qhl[:, 0, :].bitcast(F32),
                                      ALU.subtract).then_inc(s_qlo, 1)
                elif kind == "K":
                    b, c = e[1:]
                    k0, kn = KCH[c]
                    wait(s_khi, len(KCH) * b + c + 1)
                    eng.tensor_tensor(khl[:, 1, k0:k0 + kn], misc[:, 0:kn],
                                      khl[:, 0, k0:k0 + kn].bitcast(F32),
                                      ALU.subtract).then_inc(s_klo, 1)
                elif kind == "F1":
                    i = e[2]
                    wait(s_misc, misc_no[e] + 1)
                    fin = misc[:, :].rearrange("p (q c) -> p q c", c=32)
                    done(eng.reciprocal(rden[:, :], fin[:, :, DH]))
                    if i == 0 and e[1] > 0:
                        wait(s_misc, misc_no["F2", e[1] - 1] + 1)
                    eng.tensor_tensor(
                        conc[:, :, 2 * i:2 * i + 2, :, :].rearrange("p t g j e -> p t (g j) e"),
                        fin[:, :, 0:DH].rearrange("p (t h) e -> p t h e", t=NT),
                        rden[:, :].rearrange("p (t h) -> p t h", t=NT).unsqueeze(3)
                        .to_broadcast([P, NT, H // 2, DH]),
                        ALU.mult).then_inc(s_conc, 1)
                elif kind == "F3":
                    b = e[1]
                    wait(s_misc, misc_no[e] + 1)
                    wait(s_tanh, 1)
                    xb = x_sb[:, b * NT:(b + 1) * NT, :].rearrange("p t d -> p (t d)")
                    eng.scalar_tensor_tensor(xb, misc[:, 0:N], tgate[:, 0:1], xb,
                                             ALU.mult, ALU.add).then_inc(s_res, 1)
                elif kind == "R":
                    b = e[1]
                    wait(s_misc, misc_no[e] + 1)
                    eng.tensor_copy(
                        lg[:, b * NT:(b + 1) * NT, :].rearrange("p t e -> p (t e)"),
                        misc[:, 0:NT * NE]).then_inc(s_lgt, 1)
            finish_chains()

            def split_block(k):
                wait(s_xh, k + 1)
                eng.tensor_tensor(xl[:, k % 2, :], xn2T[:, k * BLK:(k + 1) * BLK],
                                  xh[:, k % 2, :].bitcast(F32), ALU.subtract).then_inc(s_xl, 1)

            def split_weights(ex):
                w = slice(ex * HID, (ex + 1) * HID)
                wait(s_wh, ex + 1)
                eng.tensor_tensor(w1l[:, w], wraw[:, ex % 2, 0, :], w1h[:, w].bitcast(F32),
                                  ALU.subtract)
                eng.tensor_tensor(w2l[:, w], wraw[:, ex % 2, 1, :], w2h[:, w].bitcast(F32),
                                  ALU.subtract).then_inc(s_wl, 1)

            split_weights(0)
            split_block(0)

            def per_tile(ap):
                return ap.unsqueeze(2).to_broadcast([P, TILES, NE])

            ranks = rank[:, :].unsqueeze(1).to_broadcast([P, TILES, NE])
            p1, p2, den, key = (top[:, n, :] for n in range(4))
            wait(s_lgt, B)
            wait(s_init, N_INIT)
            done(eng.tensor_reduce(p1, lg[:, :, :], AX.X, ALU.max))
            eng.tensor_tensor(lg[:, :, :], lg[:, :, :], per_tile(p1), ALU.subtract)\
               .then_inc(s_lg, 1)
            wait(s_w2, 16 * N_W2)
            eng.tensor_copy(ehot[:, :, :], ehot_f[:, :].unsqueeze(2).to_broadcast([2 * NE, NE, P]))
            wait(s_pe, 1)
            done(eng.tensor_reduce(den, lg[:, :, :], AX.X, ALU.add))
            done(eng.reciprocal(den, den))
            done(eng.tensor_tensor(lg[:, :, :], lg[:, :, :], per_tile(den), ALU.mult))

            def first_of_largest(value, hot):
                done(eng.tensor_reduce(value, lg[:, :, :], AX.X, ALU.max))
                done(eng.tensor_tensor(eq, lg[:, :, :], per_tile(value), ALU.is_equal))
                done(eng.tensor_tensor(eq, eq, ranks, ALU.mult))
                done(eng.tensor_reduce(key, eq, AX.X, ALU.max))
                done(eng.tensor_tensor(hot, eq, per_tile(key), ALU.is_equal))

            first_of_largest(p1, oh1)
            done(eng.scalar_tensor_tensor(lg[:, :, :], oh1, -2.0, lg[:, :, :],
                                          ALU.mult, ALU.add))
            first_of_largest(p2, cw[:, :, :])
            done(eng.tensor_tensor(den, p1, p2, ALU.add))
            done(eng.tensor_scalar(den, den, TOPK_EPS, None, ALU.add))
            done(eng.reciprocal(den, den))
            done(eng.tensor_tensor(p1, p1, den, ALU.mult))
            done(eng.tensor_tensor(p2, p2, den, ALU.mult))
            done(eng.tensor_tensor(oh1, oh1, per_tile(p1), ALU.mult))
            done(eng.tensor_tensor(cw[:, :, :], cw[:, :, :], per_tile(p2), ALU.mult))
            done(eng.tensor_tensor(cw[:, :, :], cw[:, :, :], oh1, ALU.add))
            done(eng.tensor_copy(cwhl[:, :, 0, :], cw[:, :, :]))
            eng.tensor_tensor(cwhl[:, :, 1, :], cw[:, :, :], cwhl[:, :, 0, :].bitcast(F32),
                              ALU.subtract).then_inc(s_cw, 1)

            for q in range(CHUNKS + 3 * HC):
                i, c = divmod(q, HC)
                k, ex = divmod(i, NE)
                if q < CHUNKS:
                    wait(s_hg, q + 1)
                    wait(s_f2, q - RING + 1)
                    if q % 2 == 0:
                        wait(s_hh, q // 2 + 1)
                    else:
                        done(eng.tensor_copy(hh[:, q % RING, :], hf[:, q % RING, :]))
                    eng.tensor_tensor(hl[:, q % RING, :], hf[:, q % RING, :],
                                      hh[:, q % RING, :].bitcast(F32),
                                      ALU.subtract).then_inc(s_hl, 1)
                    if c == 0 and k == 0 and ex + 1 < NE:
                        split_weights(ex + 1)
                    if c == 1 and ex == NE - 1 and k + 1 < NBLK:
                        split_block(k + 1)
                i3, c3 = divmod(q - 2 * HC, HC)
                if c3 == 0 and 0 <= i3 < NBLK * NE:
                    k3, e3 = divmod(i3, NE)
                    wait(s_f2, HC * (i3 + 1))
                    wait(s_cb, i3 + 1)
                    if e3 == 0:
                        wait(s_tp, k3 - 1)
                        dst = acc[:, k3 % 2, :]
                    else:
                        wait(s_acc, added(i3 - 2))
                        dst = yt[:, i3 % 2, :]
                    eng.scalar_tensor_tensor(dst, yp[i3 % 2][:, :], b2_sb[:, e3:e3 + 1],
                                             cwb[:, i3 % CWB, :], ALU.add, ALU.mult)\
                       .then_inc(s_yt, 1)
                if c3 == 3 and i3 >= 0 and i3 % NE == 1 and 0 < i3 // NE:
                    add_to_x(eng, wait, i3 // NE - 1)
            add_to_x(eng, wait, NBLK - 1)


N_W, N_W2 = 4, 6
N_INIT = 1 + NE

_INS = ["x", "ctxT", "gates", "wq", "wk", "wv", "woT", "rwT", "w1T", "b1T", "w2T", "b2T", "ident",
        "ehots"]


def _lay_out(i):
    a = {k: np.asarray(v) for k, v in i.items()}
    heads = lambda w: w.transpose(1, 0, 2).reshape(D, D)
    return {
        "x": a["x"].reshape(B * N, D),
        "ctxT": a["ctx_1024"].transpose(0, 2, 1),
        "gates": np.concatenate([a["g_xattn"], a["g_ffn"]]),
        "wq": heads(a["L0_xattn_Wq"]),
        "wk": heads(a["L0_xattn_Wk"]),
        "wv": heads(a["L0_xattn_Wv"]),
        "woT": a["L0_xattn_Wo"].T,
        "rwT": a["L0_ffn_router_w"].T,
        "w1T": a["L0_ffn_w1"].transpose(2, 0, 1).reshape(D, NE * HID),
        "b1T": a["L0_ffn_b1"].reshape(NE * HC, P).T,
        "w2T": a["L0_ffn_w2"].transpose(0, 2, 1).reshape(NE * HC, P, D).transpose(1, 0, 2)
        .reshape(P, NE * HID),
        "b2T": a["L0_ffn_b2"].T,
        "ident": np.eye(P, dtype=np.float32),
        "ehots": np.tile(np.eye(NE, dtype=np.float32), (2, 1)),
    }


def kernel(**inputs):
    import concourse.bacc as _bacc
    from concourse.bass_utils import run_bass_kernel_spmd as _run

    nc = _bacc.Bacc("TRN2", target_bir_lowering=False, num_devices=1)
    laid = _lay_out(inputs)
    arrays, args = {}, []
    for name in _INS:
        a = np.ascontiguousarray(laid[name])
        arrays[f"in_{name}"] = a
        args.append(nc.dram_tensor(f"in_{name}", a.shape, mybir.dt.from_np(a.dtype),
                                   kind="ExternalInput").ap())
    out = nc.dram_tensor("out_x", (B * N, D), F32, kind="ExternalOutput").ap()
    build(nc, *args, out)
    r = _run(nc, [arrays], core_ids=[0])
    return r.results[0]["out_x"].reshape(B, N, D)
```

```python
from contextlib import ExitStack

import concourse.bass as bass
import numpy as np
from concourse import mybir

F32 = mybir.dt.float32
F32R = mybir.dt.float32r
I32 = mybir.dt.int32
ALU = mybir.AluOpType
ACT = mybir.ActivationFunctionType
AX = mybir.AxisListType

B, N, D = 16, 256, 128
M = 1601
H, DH = 16, 8
NE, HID = 8, 512
P = 128
SCALE = 0.125
LN_EPS = 1e-5
TOPK_EPS = 1e-8

NT = N // P
TILES = B * NT
HG = 4
NG = H // HG
KT = -(-M // P)
UNITS = NG * KT
WIN = 402
WSTART = [0, 400, 800, M - WIN]
NW = len(WSTART)
KCH = [(0, 401), (401, 400), (801, 400), (1201, 400)]
VCH = [(0, 4), (4, 4), (8, 4), (12, 1)]
VC = DH + 1
VW = VC * (H - 1) + 32
PARTS = 3
MAXROW = PARTS * HG * DH
SCORE_ROWS = MAXROW + 2
LAG = 3
AHEAD = KT + 7
ST_BUFS = 3
MX_BUFS = 3
PT_BUFS = 8
BLK = 512
NBLK = B * N // BLK
BT = BLK // P
HC = HID // P
CHUNKS = NBLK * NE * HC
RING = 4
HP_BUFS = 3
HLAG = 3
CWB = 3
K_PART, Q_PART = (0, 1, 0), (0, 0, 1)
GUESS = float(0x5F3759DF)
NEWTON = 3


NEXT_AT = {0: ("N", "X"), 6: ("X",), 10: ("Q",), 14: ("K", 0), 16: ("K", 1), 18: ("K", 2),
           20: ("K", 3), 23: ("PK", 0), 24: ("PK", 1), 28: ("V", 0), 30: ("V", 1), 32: ("V", 2),
           34: ("V", 3), 36: ("PK", 2), 49: ("PK", 3)}
LAST_AT = {4: ("F1", 1), 8: ("F2",), 12: ("F3",), 14: ("N", "L"), 24: ("L",), 26: ("R",),
           29: ("E",)}
MOE_AT = {34: ("XS", 0), 36: ("W", 0), 39: ("W", 1), 42: ("W", 2), 45: ("W", 3)}
TAIL_AT = {1: ("F1", 1), 4: ("F2",), 6: ("F3",), 7: ("N", "L"), 14: ("L",), 16: ("R",), 18: ("E",)}
EARLY = sum(e[0] == "W" for e in MOE_AT.values())
HALF_AT, TURN_AT = 44, 9


def key_rows(kt):
    return min(P, M - kt * P)


def schedule():
    ev = []
    n_max = HG * NT * NW
    n_groups = B * NG

    def at_batch(e, b):
        return e + (b,) if e[0] == "N" else e[:1] + (b,) + e[1:]

    def last(v):
        return v % KT == KT - 1

    def maxima(v):
        windows = []
        for G, kt in (divmod(v, KT), divmod(v + 1, KT)):
            if G < n_groups:
                windows += [[("MX", G, m)] for m in range(kt * n_max // KT, (kt + 1) * n_max // KT)]
                if kt == KT - 1:
                    windows[-1].append(("MF", G))
        parts = [[] for _ in range(5)]
        for i, w in enumerate(windows):
            parts[i * 5 // len(windows)] += w
        return parts

    ev += [("N", "X", 0)] + [("K", 0, c) for c in range(len(KCH))] + [("X", 0), ("Q", 0)]
    ev += [("PK", 0, 0), ("PK", 0, 1)]
    ev += [("V", 0, c) for c in range(len(VCH))]
    for v in range(0, AHEAD, 2):
        ev += sum(maxima(v), [])
        if v == KT + 1:
            ev += [("MT", 0), ("PK", 0, 2), ("PK", 0, 3)]
    for u in range(B * UNITS):
        b, r = divmod(u, UNITS)
        G = u // KT
        if u % 2 == 0:
            parts = maxima(u + AHEAD)
        copy = [("PC", (u - LAG) // KT)] if u >= LAG and last(u - LAG) else []
        ev += copy * (u % 2) + [("S", u, 0)] + parts.pop(0)
        ev += [("S", u, 1)] + copy * (1 - u % 2) + parts.pop(0)
        if u % 2 and u >= LAG:
            ev += [("PV", v) for v in (u - LAG, u - LAG + 1) if v % 2 or not last(v)]
        elif u % 2 == 0 and u >= LAG and last(u - LAG + 1):
            ev.append(("PV", u - LAG + 1))
        if u % 2:
            ev += parts.pop(0)
        if u % KT == TURN_AT and G + 1 < n_groups:
            ev.append(("MT", G + 1))
        if b + 1 < B and r in NEXT_AT:
            ev.append(at_batch(NEXT_AT[r], b + 1))
        if b > 0 and r in LAST_AT:
            ev.append(at_batch(LAST_AT[r], b - 1))
        if r == HALF_AT:
            ev.append(("F1", b, 0))
        if b == B - 1 and r in MOE_AT:
            ev.append(MOE_AT[r])
    ev += [("PV", B * UNITS - n) for n in range(LAG - 1, 0, -1)] + [("PC", n_groups - 1)]
    return ev, {q: at_batch(e, B - 1) for q, e in TAIL_AT.items()}


def uses_shared_bank(e):
    return e[0] in ("X", "Q", "V", "MT", "F1", "F2", "F3", "L", "R") or e[0] == "K" and e[1] > 0


def build(nc, x, ctxT, gates, wq, wk, wv, woT, rwT, w1T, b1T, w2T, b2T, ident, ehots, out):
    events, tail = schedule()
    all_events = events + [tail[q] for q in sorted(tail)]
    misc_no = {}
    for e in all_events:
        if uses_shared_bank(e):
            misc_no[e] = len(misc_no)
    norms = [e[1:] for e in all_events if e[0] == "N"]
    norm_no = {e: i for i, e in enumerate(norms)}

    ctx = ExitStack()
    with ctx:
        def sb(name, shape, dt=F32):
            return ctx.enter_context(nc.sbuf_tensor(name, shape, dt))

        def sem(name):
            return ctx.enter_context(nc.semaphore(name))

        def carve(flat, sizes):
            at, parts = 0, []
            for n in sizes:
                parts.append(flat[:, at:at + n])
                at += n
            return parts

        x_sb = sb("x_sb", [P, TILES, D])
        xn2T = sb("xn2T", [P, B * N])
        kpack = sb("kpack", [P, 2, NG, M], F32R)
        khl = sb("khl", [P, 2, M], F32R)
        qmask = sb("qmask", [P, 2, NG, HG, N], F32R)
        qhl = sb("qhl", [P, 2, N], F32R)
        arena = sb("arena", [P, 2 * M + 2 * KT * VW + PT_BUFS * BLK])
        ctx_f, vaug_f, pt_f = carve(arena, [2 * M, 2 * KT * VW, PT_BUFS * BLK])
        ctx_sb = ctx_f.rearrange("p (k m) -> p k m", k=2)
        vaug = vaug_f.rearrange("p (k t w) -> p k t w", k=2, t=KT)
        pt = pt_f.rearrange("p (k n) -> p k n", k=PT_BUFS)
        hf, cwb, yt, acc = carve(arena, [RING * BLK, CWB * BLK, 2 * BLK, 2 * BLK])
        hf, cwb, yt, acc = (v.rearrange("p (k n) -> p k n", n=BLK) for v in (hf, cwb, yt, acc))
        halves = kpack[:, :, :, :].rearrange("p a g m -> p a (g m)")

        def weights(n, ex):
            at = (ex % EARLY * 3 + n) * HID
            return halves[:, ex // EARLY, at:at + HID]

        w2l, hh, hl = carve(qmask[:, :, :, :, :].rearrange("p a g j n -> p (a g j n)"),
                            [NE * HID, RING * BLK, RING * BLK])
        hh, hl = (v.rearrange("p (k n) -> p k n", n=BLK) for v in (hh, hl))
        xh, xl, cwT = carve(khl[:, :, :].rearrange("p s m -> p (s m)"), [2 * BLK] * 3)
        xh, xl, cwT = (v.rearrange("p (k n) -> p k n", n=BLK) for v in (xh, xl, cwT))

        wq_sb, wk_sb, wv_sb, wo_sb = (sb(n, [P, D]) for n in ("wq_sb", "wk_sb", "wv_sb", "wo_sb"))
        id_sb = sb("id_sb", [P, P])
        rw_sb = sb("rw_sb", [P, NE])
        wraw = sb("wraw", [P, 2, 2, HID])
        b1_sb = sb("b1_sb", [P, NE * HC])
        b2_sb = sb("b2_sb", [P, NE])
        gate = sb("gate", [P, 2])
        tgate = sb("tgate", [P, 2])
        xn = sb("xn", [P, NT, D])
        xnT = sb("xnT", [P, N])
        pv_sb = sb("pv_sb", [P, 2, BLK])
        conc = sb("conc", [P, NT, NG, HG, DH])
        concT = sb("concT", [P, N])
        rden = sb("rden", [P, NT * H // 2])
        mx = sb("mx", [P, NT * HG, NW])
        nmx = sb("nmx", [P, NT * HG])
        mxhl = sb("mxhl", [P, NT, 2, HG], F32R)
        mxT = sb("mxT", [2 * HG, N], F32R)
        bst = sb("bst", [P, NT, 6])
        stat = sb("stat", [P, NT, 2])
        var = sb("var", [P, NT])
        half = sb("half", [P, NT], I32)
        rstd = sb("rstd", [P, NT])
        tmp = sb("tmp", [P, NT])
        lg = sb("lg", [P, TILES, NE])
        cw = sb("cw", [P, NT, NE])
        cwhl = sb("cwhl", [P, TILES, 2, NE], F32R)
        eq = sb("eq", [P, NT, NE])
        oh1 = sb("oh1", [P, NT, NE])
        top = sb("top", [P, 4, NT])
        rank = sb("rank", [P, NE])
        ehot_f = sb("ehot_f", [2 * NE, NE])
        ehot = sb("ehot", [2 * NE, NE, P], F32R)

        bank = [ctx.enter_context(nc.psum_tensor(f"bank{i}", [P, BLK], F32)) for i in range(8)]
        st, mxp, pv, misc = bank[0:ST_BUFS], bank[3:3 + MX_BUFS], bank[6], bank[7]
        hp, spread, turn, yp = bank[0:HP_BUFS], bank[3], bank[4], bank[5:7]

        s_w = sem("s_w")
        s_w2 = sem("s_w2")
        s_x0 = sem("s_x0")
        s_x = sem("s_x")
        s_ctx = [sem("s_ctx0"), sem("s_ctx1")]
        s_wraw = [sem("s_wraw0"), sem("s_wraw1")]
        s_fill = sem("s_fill")
        s_init = sem("s_init")
        s_seed = sem("s_seed")
        s_pool = sem("s_pool")
        s_tanh = sem("s_tanh")
        s_xn = sem("s_xn")
        s_misc = sem("s_misc")
        s_k0 = sem("s_k0")
        s_xnT = sem("s_xnT")
        s_qhi = sem("s_qhi")
        s_qlo = sem("s_qlo")
        s_khi = sem("s_khi")
        s_klo = sem("s_klo")
        s_qd = [[sem(f"s_qd{i}{g}") for g in range(NG)] for i in range(2)]
        s_kd = [[sem(f"s_kd{i}{g}") for g in range(NG)] for i in range(2)]
        s_v = sem("s_v")
        s_mxp = sem("s_mxp")
        s_red = sem("s_red")
        s_mxhl = sem("s_mxhl")
        s_mxT = sem("s_mxT")
        s_mxd = [sem("s_mxd0"), sem("s_mxd1")]
        s_st = sem("s_st")
        s_exp = sem("s_exp")
        s_pv = sem("s_pv")
        s_pvs = sem("s_pvs")
        s_conc = sem("s_conc")
        s_concT = sem("s_concT")
        s_dve = sem("s_dve")
        s_res = sem("s_res")
        s_x2T = sem("s_x2T")
        s_lgt = sem("s_lgt")
        s_lg = sem("s_lg")
        s_pe = sem("s_pe")
        s_cw = sem("s_cw")
        s_wh = sem("s_wh")
        s_wl = sem("s_wl")
        s_xh = sem("s_xh")
        s_xl = sem("s_xl")
        s_hp = sem("s_hp")
        s_hg = sem("s_hg")
        s_hh = sem("s_hh")
        s_hl = sem("s_hl")
        s_f2 = sem("s_f2")
        s_cwp = sem("s_cwp")
        s_cwT = sem("s_cwT")
        s_cbp = sem("s_cbp")
        s_cb = sem("s_cb")
        s_yt = sem("s_yt")
        s_acc = sem("s_acc")
        s_tp = sem("s_tp")
        s_o = sem("s_o")
        s_out = sem("s_out")

        signal = {"X": s_xnT, "Q": s_qlo, "K": s_klo, "V": s_v, "MT": s_mxT, "F1": s_conc,
                  "F2": s_concT, "F3": s_res, "L": s_x2T, "R": s_lgt}
        uses = dict.fromkeys(signal, 0)
        uses["K"] = len(KCH)
        read_out = []
        for e in misc_no:
            uses[e[0]] += 1
            read_out.append((signal[e[0]], uses[e[0]]))

        block = ctx.enter_context(nc.Block())

        def waiter(eng):
            seen = {}

            def wait(s, value):
                if value > seen.get(id(s), 0):
                    seen[id(s)] = value
                    eng.wait_ge(s, value)
            return wait

        @block.sync
        def _(eng):
            wait = waiter(eng)
            xs = x.rearrange("(t p) d -> p t d", p=P)
            eng.dma_start(x_sb[:, 0:NT, :], xs[:, 0:NT, :]).then_inc(s_x0, 16)
            eng.dma_start(wk_sb[:, :], wk).then_inc(s_w, 16)
            eng.dma_start(ctx_sb[:, 0, :], ctxT[0]).then_inc(s_ctx[0], 16)
            for dst, src in ((id_sb, ident), (wq_sb, wq), (wv_sb, wv)):
                eng.dma_start(dst[:, :], src).then_inc(s_w, 16)
            eng.dma_start(x_sb[:, NT:TILES, :], xs[:, NT:TILES, :]).then_inc(s_x, 16)
            for dst, src in ((wo_sb, woT), (rw_sb, rwT), (b1_sb, b1T), (b2_sb, b2T),
                             (gate, gates.partition_broadcast(P)), (ehot_f, ehots)):
                eng.dma_start(dst[:, :], src).then_inc(s_w2, 16)
            eng.dma_start(ctx_sb[:, 1, :], ctxT[1]).then_inc(s_ctx[1], 16)

            def load_expert(ex):
                for i, w in enumerate((w1T, w2T)):
                    eng.dma_start(wraw[:, ex % 2, i, :], w[:, ex * HID:(ex + 1) * HID]
                                  ).then_inc(s_wraw[ex % 2], 16)

            def load_after(ex):
                wait(s_wh, ex + 1)
                wait(s_wl, ex + 1)
                load_expert(ex + 2)

            for e in events:
                if e[0] == "PK":
                    b, g = e[1:]
                    wait(s_klo, len(KCH) * (b + 1))
                    wait(s_st, 2 * UNITS * (b - 1))
                    for part in range(PARTS):
                        r = part * HG * DH
                        eng.dma_start(kpack[r:r + HG * DH, b % 2, g, :].bitcast(F32),
                                      khl[g * HG * DH:(g + 1) * HG * DH, K_PART[part], :]
                                      .bitcast(F32)).then_inc(s_kd[b % 2][g], 16)
                    wait(s_fill, min(1 + b, 2))
                    wait(s_qlo, b + 1)
                    for part in range(PARTS):
                        r = part * HG * DH
                        for j in range(HG):
                            h, rj = g * HG + j, r + j * DH
                            eng.dma_start(qmask[rj:rj + DH, b % 2, g, j, :].bitcast(F32),
                                          qhl[h * DH:(h + 1) * DH, Q_PART[part], :]
                                          .bitcast(F32)).then_inc(s_qd[b % 2][g], 16)
                elif e[0] == "V" and e[2] == len(VCH) - 1:
                    b = e[1]
                    if b + 2 < B:
                        wait(s_v, len(VCH) * (b + 1))
                        eng.dma_start(ctx_sb[:, b % 2, :], ctxT[b + 2]).then_inc(s_ctx[b % 2], 16)
                    if b == 0:
                        load_expert(0)
                        load_expert(1)
                elif e[0] == "MT":
                    b, g = divmod(e[1], NG)
                    wait(s_mxT, e[1] + 1)
                    for half_no in range(2):
                        eng.dma_start(
                            qmask[MAXROW + half_no:MAXROW + half_no + 1, b % 2, g, :, :]
                            .bitcast(F32),
                            mxT[half_no * HG:(half_no + 1) * HG, :].bitcast(F32)
                        ).then_inc(s_mxd[e[1] % 2], 16)
                elif e[0] == "W":
                    load_after(e[1])
            for ex in range(EARLY, NE - 2):
                load_after(ex)
            outs = out.rearrange("(t p) d -> p t d", p=P)
            for k in range(NBLK):
                wait(s_o, k + 1)
                eng.dma_start(outs[:, k * BT:(k + 1) * BT, :],
                              x_sb[:, k * BT:(k + 1) * BT, :]).then_inc(s_out, 16)
            eng.wait_ge(s_out, 16 * NBLK)

        @block.gpsimd
        def _(eng):
            wait = waiter(eng)
            own = [0]

            def done(ins):
                ins.then_inc(s_pool, 1)
                own[0] += 1
                eng.wait_ge(s_pool, own[0])

            def zero_half(i):
                eng.memset(qmask[:, i, :, :, :].bitcast(F32), 0.0).then_inc(s_fill, 1)
                wait(s_fill, i + 1)

            zero_half(0)
            for e in all_events:
                if e[0] == "W":
                    wait(s_st, 2 * UNITS * (B - 1))
                    ex = e[1]
                    wait(s_wraw[ex % 2], 32 * (ex // 2 + 1))
                    eng.tensor_copy(weights(0, ex), wraw[:, ex % 2, 0, :])
                    eng.tensor_copy(weights(2, ex), wraw[:, ex % 2, 1, :]).then_inc(s_wh, 1)
                elif e[0] == "XS":
                    for g in range(NG):
                        wait(s_kd[(B - 1) % 2][g], 16 * PARTS * ((B - 1) // 2 + 1))
                    wait(s_x2T, BT // NT)
                    eng.tensor_copy(xh[:, 0, :], xn2T[:, 0:BLK]).then_inc(s_xh, 1)
                if e[0] != "N":
                    continue
                if e[1:] == ("X", 1):
                    zero_half(1)
                    eng.memset(kpack[MAXROW:P, :, :, :].bitcast(F32), 1.0).then_inc(s_fill, 1)
                    wait(s_fill, 3)
                _, which, b = e
                i = norm_no[which, b]
                wait(s_seed, i + 1)
                for _ in range(NEWTON):
                    done(eng.tensor_tensor(tmp[:, :], rstd[:, :], rstd[:, :], ALU.mult))
                    done(eng.tensor_tensor(tmp[:, :], tmp[:, :], var[:, :], ALU.mult))
                    done(eng.tensor_scalar(tmp[:, :], tmp[:, :], -0.5, 1.5, ALU.mult, ALU.add))
                    done(eng.tensor_tensor(rstd[:, :], rstd[:, :], tmp[:, :], ALU.mult))
                if i > 0:
                    wait(s_misc, misc_no[norms[i - 1]] + 1)
                for t in range(NT):
                    eng.tensor_scalar(xn[:, t, :], x_sb[:, b * NT + t, :], stat[:, t, 0:1],
                                      rstd[:, t:t + 1], ALU.subtract, ALU.mult).then_inc(s_xn, 1)
            n = 0
            for i in range(NBLK * NE):
                k, ex = divmod(i, NE)
                wait(s_yt, i + 1)
                if ex > 0:
                    wait(s_acc, n)
                    eng.tensor_tensor(acc[:, k % 2, :], acc[:, k % 2, :], yt[:, i % 2, :],
                                      ALU.add).then_inc(s_acc, 1)
                    n += 1

        @block.tensor
        def _(eng):
            wait = waiter(eng)

            def misc_bank(e):
                if misc_no[e]:
                    wait(*read_out[misc_no[e] - 1])

            n_mx = 0
            wait(s_w, 16 * N_W)

            def attend(e):
                nonlocal n_mx
                kind = e[0]
                if kind == "S":
                    u, p = e[1:]
                    b, r = divmod(u, UNITS)
                    g, kt = divmod(r, KT)
                    G, c, n = b * NG + g, 2 * u + p, key_rows(kt)
                    wait(s_fill, 3)
                    wait(s_mxd[G % 2], 32 * (G // 2 + 1))
                    wait(s_exp, c - ST_BUFS + 1)
                    eng.matmul(st[c % ST_BUFS][0:n, :],
                               kpack[0:SCORE_ROWS, b % 2, g, kt * P:kt * P + n],
                               qmask[0:SCORE_ROWS, b % 2, g, 2 * p:2 * p + 2, :],
                               start=True, stop=True).then_inc(s_st, 1)
                elif kind == "MX":
                    G, m = e[1:]
                    b, g = divmod(G, NG)
                    tj, w = divmod(m, NW)
                    t, j = divmod(tj, HG)
                    if m == 0:
                        wait(s_qd[b % 2][g], 16 * PARTS * HG * (b // 2 + 1))
                        wait(s_kd[b % 2][g], 16 * PARTS * (b // 2 + 1))
                    wait(s_red, n_mx - MX_BUFS + 1)
                    eng.matmul(mxp[n_mx % MX_BUFS][:, 0:WIN],
                               qmask[0:MAXROW, b % 2, g, j, t * P:(t + 1) * P],
                               kpack[0:MAXROW, b % 2, g, WSTART[w]:WSTART[w] + WIN],
                               start=True, stop=True).then_inc(s_mxp, 1)
                    n_mx += 1
                elif kind == "MT":
                    misc_bank(e)
                    wait(s_mxhl, e[1] + 1)
                    for t in range(NT):
                        ins = eng.transpose(
                            misc[0:2 * HG, t * P:(t + 1) * P],
                            mxhl[:, t, :, :].rearrange("p s j -> p (s j)").bitcast(F32), id_sb[:, :])
                    ins.then_inc(s_misc, 1)
                elif kind == "PV":
                    u = e[1]
                    b, r = divmod(u, UNITS)
                    g, kt = divmod(r, KT)
                    n = key_rows(kt)
                    wait(s_v, len(VCH) * (b + 1))
                    wait(s_pvs, b * NG + g)
                    for j in range(HG):
                        if j % 2 == 0:
                            wait(s_exp, 2 * u + j // 2 + 1)
                        h = g * HG + j
                        ins = eng.matmul(
                            pv[32 * j:32 * j + 32, (g % 2) * N:(g % 2 + 1) * N],
                            vaug[0:n, b % 2, kt, VC * h:VC * h + 32],
                            pt[0:n, (2 * u + j // 2) % PT_BUFS, (j % 2) * N:(j % 2 + 1) * N],
                            start=(kt == 0), stop=(kt == KT - 1), tile_position=(0, 32 * j))
                    ins.then_inc(s_pv, 1)
                elif kind in ("X", "L"):
                    misc_bank(e)
                    wait(s_xn, NT * (norm_no[e] + 1))
                    for t in range(NT):
                        ins = eng.transpose(misc[:, t * P:(t + 1) * P], xn[:, t, :], id_sb[:, :])
                    ins.then_inc(s_misc, 1)
                elif kind == "Q":
                    misc_bank(e)
                    wait(s_xnT, e[1] + 1)
                    eng.matmul(misc[:, 0:N], wq_sb[:, :], xnT[:, :],
                               start=True, stop=True).then_inc(s_misc, 1)
                elif kind == "K":
                    b, c = e[1:]
                    k0, kn = KCH[c]
                    if b > 0:
                        misc_bank(e)
                    wait(s_ctx[b % 2], 16 * (b // 2 + 1))
                    dst = misc if b > 0 else bank[c]
                    eng.matmul(dst[:, 0:kn], wk_sb[:, :], ctx_sb[:, b % 2, k0:k0 + kn],
                               start=True, stop=True).then_inc(s_misc if b > 0 else s_k0, 1)
                elif kind == "V":
                    b, c = e[1:]
                    misc_bank(e)
                    t0, tn = VCH[c]
                    for i in range(tn):
                        n = key_rows(t0 + i)
                        ins = eng.matmul(misc[0:n, i * D:(i + 1) * D],
                                         ctx_sb[:, b % 2, (t0 + i) * P:(t0 + i) * P + n],
                                         wv_sb[:, :], start=True, stop=True)
                    ins.then_inc(s_misc, 1)
                elif kind == "F1":
                    b, i = e[1:]
                    misc_bank(e)
                    wait(s_pvs, b * NG + 2 * i + 2)
                    for q in range(2 * NT):
                        at = q % NT * 2 + q // NT
                        ins = eng.transpose(misc[:, at * P:(at + 1) * P],
                                            pv_sb[:, i, q * P:(q + 1) * P], id_sb[:, :])
                    ins.then_inc(s_misc, 1)
                elif kind == "F2":
                    misc_bank(e)
                    wait(s_conc, 2 * (e[1] + 1))
                    for t in range(NT):
                        ins = eng.transpose(misc[:, t * P:(t + 1) * P],
                                            conc[:, t, :, :, :].rearrange("p g j e -> p (g j e)"),
                                            id_sb[:, :])
                    ins.then_inc(s_misc, 1)
                elif kind == "R":
                    b = e[1]
                    misc_bank(e)
                    wait(s_x2T, b + 1)
                    for t in range(NT):
                        i = b * NT + t
                        ins = eng.matmul(misc[:, t * NE:(t + 1) * NE], xn2T[:, i * P:(i + 1) * P],
                                         rw_sb[:, :], start=True, stop=True)
                    ins.then_inc(s_misc, 1)
                elif kind == "F3":
                    misc_bank(e)
                    wait(s_concT, e[1] + 1)
                    wait(s_w2, 16 * N_W2)
                    for t in range(NT):
                        ins = eng.matmul(misc[:, t * P:(t + 1) * P], concT[:, t * P:(t + 1) * P],
                                         wo_sb[:, :], start=True, stop=True)
                    ins.then_inc(s_misc, 1)

            for e in events:
                attend(e)

            wait(s_exp, 2 * B * UNITS)
            wait(s_red, n_mx)
            wait(s_pvs, B * NG)

            def weight_rows(k):
                wait(s_cw, BT // NT * (k + 1))
                wait(s_o, k - 1)
                wait(s_cwT, k)
                for t in range(BT):
                    ins = eng.transpose(
                        turn[0:2 * NE, t * P:(t + 1) * P],
                        cwhl[:, k * BT + t, :, :].rearrange("p s e -> p (s e)").bitcast(F32),
                        id_sb[:, :])
                ins.then_inc(s_cwp, 1)

            def spread_weights(i):
                k, ex = divmod(i, NE)
                wait(s_cwT, k + 1)
                wait(s_cb, i)
                eng.matmul(spread[:, :], ehot[:, ex, :], cwT[0:2 * NE, k % 2, :],
                           start=True, stop=True).then_inc(s_cbp, 1)

            def turn_back(k):
                wait(s_acc, (NE - 1) * (k + 1))
                wait(s_cwT, min(k + 2, NBLK))
                for t in range(BT):
                    ins = eng.transpose(turn[:, t * P:(t + 1) * P],
                                        acc[:, k % 2, t * P:(t + 1) * P], id_sb[:, :])
                ins.then_inc(s_tp, 1)

            for q in range(CHUNKS + HLAG + 2 * HC):
                i, c = divmod(q, HC)
                if q < CHUNKS:
                    k, ex = divmod(i, NE)
                    w = slice(c * P, (c + 1) * P)
                    w1h, w1l = weights(0, ex)[:, w], weights(1, ex)[:, w]
                    if k == 0 and c == 0:
                        wait(s_wh, ex + 1)
                        wait(s_wl, ex + 1)
                    wait(s_xh, k + 1)
                    wait(s_xl, k + 1)
                    wait(s_hg, q - HP_BUFS + 1)
                    pairs = ((w1h, xh), (w1h, xl), (w1l, xh))
                    for n, (lhs, rhs) in enumerate(pairs):
                        ins = eng.matmul(hp[q % HP_BUFS][:, :], lhs, rhs[:, k % 2, :],
                                         start=(n == 0), stop=(n == 2))
                    ins.then_inc(s_hp, 1)
                f = q - HLAG
                if 0 <= f < CHUNKS:
                    i2, c2 = divmod(f, HC)
                    ex2 = i2 % NE
                    w2 = (weights(2, ex2)[:, c2 * P:(c2 + 1) * P],
                          w2l[:, (ex2 * HC + c2) * P:(ex2 * HC + c2 + 1) * P])
                    wait(s_hl, f + 1)
                    if c2 == 0:
                        wait(s_yt, i2 - 1)
                    for n, (lhs, rhs) in enumerate(((w2[0], hh), (w2[0], hl), (w2[1], hh))):
                        ins = eng.matmul(yp[i2 % 2][:, :], lhs, rhs[:, f % RING, :],
                                         start=(c2 == 0 and n == 0),
                                         stop=(c2 == HC - 1 and n == 2))
                    ins.then_inc(s_f2, 1)
                i3, c3 = divmod(q - 2 * HC + 1, HC)
                if c3 == 0 and 0 <= i3 < NBLK * NE:
                    if i3 == 0:
                        weight_rows(0)
                    spread_weights(i3)
                if c3 == 2 and i3 >= 0:
                    k3, e3 = divmod(i3, NE)
                    if e3 == 5 and k3 + 1 < NBLK:
                        weight_rows(k3 + 1)
                    if e3 == 1 and k3 > 0:
                        turn_back(k3 - 1)
                if q in tail:
                    attend(tail[q])
            turn_back(NBLK - 1)

        @block.scalar
        def _(eng):
            wait = waiter(eng)

            def packed(b):
                for g in range(NG):
                    wait(s_kd[b % 2][g], 16 * PARTS * (b // 2 + 1))

            def attend(e):
                kind = e[0]
                if kind == "S":
                    u, p = e[1:]
                    c, n = 2 * u + p, key_rows(u % KT)
                    wait(s_st, c + 1)
                    wait(s_pv, (c - PT_BUFS) // 2 + 1)
                    eng.activation(pt[0:n, c % PT_BUFS, :], st[c % ST_BUFS][0:n, :], ACT.Exp,
                                   scale=SCALE).then_inc(s_exp, 1)
                elif kind == "PC":
                    b, g = divmod(e[1], NG)
                    wait(s_pv, KT * (e[1] + 1))
                    if b > 0:
                        wait(s_misc, misc_no["F1", b - 1, g // 2] + 1)
                    cols = slice(g % 2 * N, (g % 2 + 1) * N)
                    eng.activation(pv_sb[:, g // 2, cols], pv[:, cols], ACT.Copy).then_inc(s_pvs, 1)
                elif kind == "X":
                    wait(s_misc, misc_no[e] + 1)
                    eng.activation(xnT[:, :], misc[:, 0:N], ACT.Copy).then_inc(s_xnT, 1)
                elif kind == "L":
                    wait(s_misc, misc_no[e] + 1)
                    eng.activation(xn2T[:, e[1] * N:(e[1] + 1) * N], misc[:, 0:N],
                                   ACT.Copy).then_inc(s_x2T, 1)
                elif kind == "Q":
                    b = e[1]
                    wait(s_misc, misc_no[e] + 1)
                    if b > 0:
                        for g in range(NG):
                            wait(s_qd[(b - 1) % 2][g], 16 * PARTS * HG * ((b - 1) // 2 + 1))
                    eng.activation(qhl[:, 0, :], misc[:, 0:N], ACT.Copy).then_inc(s_qhi, 1)
                elif kind == "K":
                    b, c = e[1:]
                    k0, kn = KCH[c]
                    if b > 0:
                        wait(s_misc, misc_no[e] + 1)
                        packed(b - 1)
                    else:
                        wait(s_k0, c + 1)
                    src = misc if b > 0 else bank[c]
                    eng.activation(khl[:, 0, k0:k0 + kn], src[:, 0:kn], ACT.Copy).then_inc(s_khi, 1)
                elif kind == "V":
                    b, c = e[1:]
                    t0, tn = VCH[c]
                    n = key_rows(t0 + tn - 1)
                    wait(s_misc, misc_no[e] + 1)
                    wait(s_pv, UNITS * (b - 1))
                    if b == 0:
                        wait(s_init, N_INIT)
                    eng.activation(
                        vaug[0:n, b % 2, t0:t0 + tn, 0:VC * H]
                        .rearrange("p t (h c) -> p t h c", c=VC)[:, :, :, 0:DH],
                        misc[0:n, 0:tn * D].rearrange("p (t h e) -> p t h e", t=tn, e=DH),
                        ACT.Copy).then_inc(s_v, 1)
                elif kind == "MT":
                    G = e[1]
                    wait(s_misc, misc_no[e] + 1)
                    if G > 0:
                        wait(s_mxd[(G - 1) % 2], 32 * ((G - 1) // 2 + 1))
                    eng.activation(mxT[:, :], misc[0:2 * HG, 0:N], ACT.Copy).then_inc(s_mxT, 1)
                elif kind == "F2":
                    wait(s_misc, misc_no[e] + 1)
                    eng.activation(concT[:, :], misc[:, 0:N], ACT.Copy).then_inc(s_concT, 1)
                elif kind == "N" and e[1:] == ("X", 1):
                    wait(s_w2, 16 * N_W2)
                    eng.activation(tgate[:, :], gate[:, :], ACT.Tanh).then_inc(s_tanh, 1)
                elif kind == "E":
                    b = e[1]
                    l_b = lg[:, b * NT:(b + 1) * NT, :]
                    wait(s_lg, b + 1)
                    eng.activation(l_b, l_b, ACT.Exp).then_inc(s_pe, 1)

            def split_block(k):
                wait(s_hp, HC * NE * (k - 1))
                eng.activation(xh[:, k % 2, :], xn2T[:, k * BLK:(k + 1) * BLK],
                               ACT.Copy).then_inc(s_xh, 1)

            def split_weights(ex):
                wait(s_wraw[ex % 2], 32 * (ex // 2 + 1))
                eng.activation(weights(0, ex), wraw[:, ex % 2, 0, :], ACT.Copy)
                eng.activation(weights(2, ex), wraw[:, ex % 2, 1, :], ACT.Copy).then_inc(s_wh, 1)

            for e in events:
                attend(e)

            wait(s_pv, B * UNITS)
            for q in range(CHUNKS + 2 * HC):
                i, c = divmod(q, HC)
                k, ex = divmod(i, NE)
                if q < CHUNKS:
                    wait(s_hp, q + 1)
                    wait(s_hl, q - RING + 1)
                    eng.activation(hf[:, q % RING, :], hp[q % HP_BUFS][:, :], ACT.Gelu_apprx_tanh,
                                   bias=b1_sb[:, ex * HC + c:ex * HC + c + 1]).then_inc(s_hg, 1)
                    if q % 2 == 0:
                        wait(s_hg, q + 1)
                        wait(s_f2, q - RING + 1)
                        eng.activation(hh[:, q % RING, :], hf[:, q % RING, :],
                                       ACT.Copy).then_inc(s_hh, 1)
                    if c == 0 and k == 0 and EARLY <= ex + 1 < NE:
                        split_weights(ex + 1)
                    if c == 1 and ex == NE - 1 and k + 1 < NBLK:
                        split_block(k + 1)
                i3, c3 = divmod(q - 2 * HC + 1, HC)
                if c3 == 0 and 0 <= i3 < NBLK * NE:
                    if i3 == 0:
                        wait(s_cwp, 1)
                        eng.activation(cwT[0:2 * NE, 0, :], turn[0:2 * NE, :],
                                       ACT.Copy).then_inc(s_cwT, 1)
                    wait(s_cbp, i3 + 1)
                    wait(s_yt, i3 - CWB + 1)
                    eng.activation(cwb[:, i3 % CWB, :], spread[:, :], ACT.Copy).then_inc(s_cb, 1)
                if c3 == 2 and i3 >= 0:
                    k3, e3 = divmod(i3, NE)
                    if e3 == 5 and k3 + 1 < NBLK:
                        wait(s_cwp, k3 + 2)
                        wait(s_cbp, NE * k3)
                        eng.activation(cwT[0:2 * NE, (k3 + 1) % 2, :], turn[0:2 * NE, :],
                                       ACT.Copy).then_inc(s_cwT, 1)
                if q in tail:
                    attend(tail[q])

        @block.vector
        def _(eng):
            wait = waiter(eng)
            own = [0]

            def done(ins):
                ins.then_inc(s_dve, 1)
                own[0] += 1
                eng.wait_ge(s_dve, own[0])

            def added(i):
                return 0 if i < 0 else (i // NE) * (NE - 1) + i % NE

            def add_to_x(k):
                wait(s_tp, k + 1)
                xb = x_sb[:, k * BT:(k + 1) * BT, :].rearrange("p t d -> p (t d)")
                eng.scalar_tensor_tensor(xb, turn[:, :], tgate[:, 1:2], xb,
                                         ALU.mult, ALU.add).then_inc(s_o, 1)

            def after_own(ins):
                ins.then_inc(s_dve, 1)
                own[0] += 1

            def own_steps():
                eng.wait_ge(s_dve, own[0])

            chains, background = [], []

            def advance(queue):
                if queue and next(queue[0], "over") == "over":
                    queue.pop(0)

            def finish(queue):
                while queue:
                    advance(queue)

            def split_maxima():
                own_steps()
                neg = nmx[:, :].rearrange("p (t j) -> p t j", t=NT)
                after_own(eng.tensor_copy(mxhl[:, :, 0, :], neg))
                yield
                own_steps()
                eng.tensor_tensor(mxhl[:, :, 1, :], neg, mxhl[:, :, 0, :].bitcast(F32),
                                  ALU.subtract).then_inc(s_mxhl, 1)
                yield

            def norm_steps(which, b):
                if which == "X":
                    wait(s_x if b else s_x0, 16)
                else:
                    wait(s_res, b + 1)
                wait(s_xn, NT * norm_no[which, b])
                for t in range(NT):
                    after_own(eng.bn_stats(bst[:, t, :], x_sb[:, b * NT + t, :]))
                yield
                own_steps()
                for t in range(NT):
                    after_own(eng.bn_aggr(stat[:, t, :], bst[:, t, :]))
                yield
                own_steps()
                after_own(eng.tensor_scalar(var[:, :], stat[:, :, 1], LN_EPS, None, ALU.add))
                yield
                own_steps()
                after_own(eng.tensor_scalar(half[:, :], var[:, :].bitcast(I32), 1, None,
                                            ALU.logical_shift_right))
                yield
                own_steps()
                eng.tensor_scalar(rstd[:, :].bitcast(I32), half[:, :], -1.0, GUESS,
                                  ALU.mult, ALU.add).then_inc(s_seed, 1)
                yield

            def per_tile(ap):
                return ap.unsqueeze(2).to_broadcast([P, NT, NE])

            ranks = rank[:, :].unsqueeze(1).to_broadcast([P, NT, NE])
            p1, p2, den, key = (top[:, n, :] for n in range(4))

            def logit_steps(b):
                l_b = lg[:, b * NT:(b + 1) * NT, :]
                own_steps()
                after_own(eng.tensor_reduce(p1, l_b, AX.X, ALU.max))
                yield
                own_steps()
                eng.tensor_tensor(l_b, l_b, per_tile(p1), ALU.subtract).then_inc(s_lg, 1)
                yield

            def routing_steps(b):
                l_b = lg[:, b * NT:(b + 1) * NT, :]
                cwhl_b = cwhl[:, b * NT:(b + 1) * NT, :, :]
                wait(s_pe, b + 1)

                def first_of_largest(value, hot):
                    return (lambda: eng.tensor_reduce(value, l_b, AX.X, ALU.max),
                            lambda: eng.tensor_tensor(eq[:, :, :], l_b, per_tile(value),
                                                      ALU.is_equal),
                            lambda: eng.tensor_tensor(eq[:, :, :], eq[:, :, :], ranks, ALU.mult),
                            lambda: eng.tensor_reduce(key, eq[:, :, :], AX.X, ALU.max),
                            lambda: eng.tensor_tensor(hot, eq[:, :, :], per_tile(key),
                                                      ALU.is_equal))

                one, two = oh1[:, :, :], cw[:, :, :]
                steps = (
                    lambda: eng.tensor_reduce(den, l_b, AX.X, ALU.add),
                    lambda: eng.reciprocal(den, den),
                    lambda: eng.tensor_tensor(l_b, l_b, per_tile(den), ALU.mult),
                    *first_of_largest(p1, one),
                    lambda: eng.scalar_tensor_tensor(l_b, one, -2.0, l_b, ALU.mult, ALU.add),
                    *first_of_largest(p2, two),
                    lambda: eng.tensor_tensor(den, p1, p2, ALU.add),
                    lambda: eng.tensor_scalar(den, den, TOPK_EPS, None, ALU.add),
                    lambda: eng.reciprocal(den, den),
                    lambda: eng.tensor_tensor(p1, p1, den, ALU.mult),
                    lambda: eng.tensor_tensor(p2, p2, den, ALU.mult),
                    lambda: eng.tensor_tensor(one, one, per_tile(p1), ALU.mult),
                    lambda: eng.tensor_tensor(two, two, per_tile(p2), ALU.mult),
                    lambda: eng.tensor_tensor(two, two, one, ALU.add),
                    lambda: eng.tensor_copy(cwhl_b[:, :, 0, :], two))
                for step in steps:
                    own_steps()
                    after_own(step())
                    yield
                own_steps()
                eng.tensor_tensor(cwhl_b[:, :, 1, :], two, cwhl_b[:, :, 0, :].bitcast(F32),
                                  ALU.subtract).then_inc(s_cw, 1)
                yield

            n_mx = 0

            def attend(e):
                nonlocal n_mx
                kind = e[0]
                if kind in ("MT", "X", "L", "E"):
                    finish(chains)
                if kind == "MX":
                    G, m = e[1:]
                    tj, w = divmod(m, NW)
                    wait(s_mxp, n_mx + 1)
                    if m == 0:
                        own_steps()
                    eng.tensor_reduce(mx[:, tj, w:w + 1], mxp[n_mx % MX_BUFS][:, 0:WIN],
                                      AX.X, ALU.max).then_inc(s_red, 1)
                    n_mx += 1
                    advance(chains or background)
                elif kind == "MF":
                    G = e[1]
                    finish(chains)
                    wait(s_red, n_mx)
                    if G > 0:
                        wait(s_misc, misc_no[("MT", G - 1)] + 1)
                    after_own(eng.tensor_reduce(nmx[:, :], mx[:, :, :], AX.X, ALU.max,
                                                negate=True))
                    chains.append(split_maxima())
                elif kind == "N":
                    finish(chains)
                    chains.append(norm_steps(*e[1:]))
                    if e[1:] in (("X", 0), ("L", B - 1)):
                        finish(chains)
                    if e[1:] == ("X", 0):
                        eng.memset(vaug, 1.0).then_inc(s_init, 1)
                        for ex in range(NE):
                            eng.memset(rank[:, ex:ex + 1], float(NE - ex)).then_inc(s_init, 1)
                elif kind == "Q":
                    wait(s_qhi, e[1] + 1)
                    eng.tensor_tensor(qhl[:, 1, :], misc[:, 0:N], qhl[:, 0, :].bitcast(F32),
                                      ALU.subtract).then_inc(s_qlo, 1)
                elif kind == "K":
                    b, c = e[1:]
                    k0, kn = KCH[c]
                    wait(s_khi, len(KCH) * b + c + 1)
                    src = misc if b > 0 else bank[c]
                    eng.tensor_tensor(khl[:, 1, k0:k0 + kn], src[:, 0:kn],
                                      khl[:, 0, k0:k0 + kn].bitcast(F32),
                                      ALU.subtract).then_inc(s_klo, 1)
                elif kind == "F1":
                    i = e[2]
                    wait(s_misc, misc_no[e] + 1)
                    fin = misc[:, :].rearrange("p (q c) -> p q c", c=32)
                    done(eng.reciprocal(rden[:, :], fin[:, :, DH]))
                    if i == 0 and e[1] > 0:
                        wait(s_misc, misc_no["F2", e[1] - 1] + 1)
                    eng.tensor_tensor(
                        conc[:, :, 2 * i:2 * i + 2, :, :].rearrange("p t g j e -> p t (g j) e"),
                        fin[:, :, 0:DH].rearrange("p (t h) e -> p t h e", t=NT),
                        rden[:, :].rearrange("p (t h) -> p t h", t=NT).unsqueeze(3)
                        .to_broadcast([P, NT, H // 2, DH]),
                        ALU.mult).then_inc(s_conc, 1)
                elif kind == "F3":
                    b = e[1]
                    wait(s_misc, misc_no[e] + 1)
                    wait(s_tanh, 1)
                    xb = x_sb[:, b * NT:(b + 1) * NT, :].rearrange("p t d -> p (t d)")
                    eng.scalar_tensor_tensor(xb, misc[:, 0:N], tgate[:, 0:1], xb,
                                             ALU.mult, ALU.add).then_inc(s_res, 1)
                elif kind == "R":
                    b = e[1]
                    wait(s_misc, misc_no[e] + 1)
                    eng.tensor_copy(
                        lg[:, b * NT:(b + 1) * NT, :].rearrange("p t e -> p (t e)"),
                        misc[:, 0:NT * NE]).then_inc(s_lgt, 1)
                    wait(s_init, N_INIT)
                    wait(s_lgt, b + 1)
                    finish(background)
                    chains.append(logit_steps(b))
                elif kind == "E":
                    background.append(routing_steps(e[1]))
                elif kind == "W":
                    split_weights(e[1])
                elif kind == "XS":
                    split_block(e[1])
                    wait(s_w2, 16 * N_W2)
                    done(eng.tensor_copy(ehot[:, :, :],
                                         ehot_f[:, :].unsqueeze(2).to_broadcast([2 * NE, NE, P])))
            def split_block(k):
                wait(s_xh, k + 1)
                eng.tensor_tensor(xl[:, k % 2, :], xn2T[:, k * BLK:(k + 1) * BLK],
                                  xh[:, k % 2, :].bitcast(F32), ALU.subtract).then_inc(s_xl, 1)

            def split_weights(ex):
                wait(s_wh, ex + 1)
                eng.tensor_tensor(weights(1, ex), wraw[:, ex % 2, 0, :],
                                  weights(0, ex).bitcast(F32), ALU.subtract)
                eng.tensor_tensor(w2l[:, ex * HID:(ex + 1) * HID], wraw[:, ex % 2, 1, :],
                                  weights(2, ex).bitcast(F32), ALU.subtract).then_inc(s_wl, 1)

            for e in events:
                attend(e)
            finish(chains)

            for q in range(CHUNKS + 3 * HC):
                i, c = divmod(q, HC)
                k, ex = divmod(i, NE)
                if q < CHUNKS:
                    wait(s_hg, q + 1)
                    wait(s_f2, q - RING + 1)
                    if q % 2 == 0:
                        wait(s_hh, q // 2 + 1)
                    else:
                        done(eng.tensor_copy(hh[:, q % RING, :], hf[:, q % RING, :]))
                    eng.tensor_tensor(hl[:, q % RING, :], hf[:, q % RING, :],
                                      hh[:, q % RING, :].bitcast(F32),
                                      ALU.subtract).then_inc(s_hl, 1)
                    if c == 0 and k == 0 and EARLY <= ex + 1 < NE:
                        split_weights(ex + 1)
                    if c == 1 and ex == NE - 1 and k + 1 < NBLK:
                        split_block(k + 1)
                i3, c3 = divmod(q - 2 * HC, HC)
                if c3 == 0 and 0 <= i3 < NBLK * NE:
                    k3, e3 = divmod(i3, NE)
                    wait(s_f2, HC * (i3 + 1))
                    wait(s_cb, i3 + 1)
                    if e3 == 0:
                        wait(s_tp, k3 - 1)
                        dst = acc[:, k3 % 2, :]
                    else:
                        wait(s_acc, added(i3 - 2))
                        dst = yt[:, i3 % 2, :]
                    eng.scalar_tensor_tensor(dst, yp[i3 % 2][:, :], b2_sb[:, e3:e3 + 1],
                                             cwb[:, i3 % CWB, :], ALU.add, ALU.mult)\
                       .then_inc(s_yt, 1)
                if c3 == 3 and i3 >= 0 and i3 % NE == 1 and 0 < i3 // NE:
                    add_to_x(i3 // NE - 1)
                if q in tail:
                    attend(tail[q])
                advance(chains or background)
            add_to_x(NBLK - 1)


N_W, N_W2 = 4, 6
N_INIT = 1 + NE

_INS = ["x", "ctxT", "gates", "wq", "wk", "wv", "woT", "rwT", "w1T", "b1T", "w2T", "b2T", "ident",
        "ehots"]


def _lay_out(i):
    a = {k: np.asarray(v) for k, v in i.items()}
    heads = lambda w: w.transpose(1, 0, 2).reshape(D, D)
    return {
        "x": a["x"].reshape(B * N, D),
        "ctxT": a["ctx_1024"].transpose(0, 2, 1),
        "gates": np.concatenate([a["g_xattn"], a["g_ffn"]]),
        "wq": heads(a["L0_xattn_Wq"]),
        "wk": heads(a["L0_xattn_Wk"]),
        "wv": heads(a["L0_xattn_Wv"]),
        "woT": a["L0_xattn_Wo"].T,
        "rwT": a["L0_ffn_router_w"].T,
        "w1T": a["L0_ffn_w1"].transpose(2, 0, 1).reshape(D, NE * HID),
        "b1T": a["L0_ffn_b1"].reshape(NE * HC, P).T,
        "w2T": a["L0_ffn_w2"].transpose(0, 2, 1).reshape(NE * HC, P, D).transpose(1, 0, 2)
        .reshape(P, NE * HID),
        "b2T": a["L0_ffn_b2"].T,
        "ident": np.eye(P, dtype=np.float32),
        "ehots": np.tile(np.eye(NE, dtype=np.float32), (2, 1)),
    }


def kernel(**inputs):
    import concourse.bacc as _bacc
    from concourse.bass_utils import run_bass_kernel_spmd as _run

    nc = _bacc.Bacc("TRN2", target_bir_lowering=False, num_devices=1)
    laid = _lay_out(inputs)
    arrays, args = {}, []
    for name in _INS:
        a = np.ascontiguousarray(laid[name])
        arrays[f"in_{name}"] = a
        args.append(nc.dram_tensor(f"in_{name}", a.shape, mybir.dt.from_np(a.dtype),
                                   kind="ExternalInput").ap())
    out = nc.dram_tensor("out_x", (B * N, D), F32, kind="ExternalOutput").ap()
    build(nc, *args, out)
    r = _run(nc, [arrays], core_ids=[0])
    return r.results[0]["out_x"].reshape(B, N, D)
```
